# Optimizing a Trainium2 kernel written in Bass

```python
import numpy as np
import jax
import jax.numpy as jnp

def _softmax(x, axis=-1):
    return jax.nn.softmax(x, axis=axis)

def _gelu(x):
    return jax.nn.gelu(x, approximate=True)

def _silu(x):
    return jax.nn.silu(x)

def _sigmoid(x):
    return jax.nn.sigmoid(x)

def _layernorm(x, axis=-1, eps=1e-05):
    m = jnp.mean(x, axis=axis, keepdims=True)
    v = jnp.var(x, axis=axis, keepdims=True)
    return (x - m) / jnp.sqrt(v + eps)

def _scatter_add(tgt, idx, src, axis=0):
    return tgt.at[idx].add(src)

def _segment_sum(src, seg, n):
    return jax.ops.segment_sum(src, seg, n)
kernel_name = 'mk_sandwich_d1_jaxref_r8_63c741'

def setup_inputs(seed: int=0):
    np.random.seed(seed)
    _w = jnp.asarray

    def _L0_attn_setup():
        import jax, jax.numpy as jnp
        import numpy as np
        B, N, D = (2, 256, 128)
        H = 16
        HD = D // H
        ROPE_BASE = 10000.0

        def _rotate_half(t):
            t = t.reshape(*t.shape[:-1], -1, 2)
            x1, x2 = (t[..., 0], t[..., 1])
            return jnp.stack((-x2, x1), axis=-1).reshape(*t.shape[:-2], -1)

        def _apply_rope(t, cos, sin):
            return t * cos + _rotate_half(t) * sin
        key = jax.random.key(seed)
        ks = jax.random.split(key, 5)
        s = 0.02
        return {'x': jax.random.normal(ks[0], (B, N, D), dtype=jnp.float32), 'qkv_w': jax.random.normal(ks[1], (3 * D, D), dtype=jnp.float32) * s, 'qkv_b': jax.random.normal(ks[2], (3 * D,), dtype=jnp.float32) * s, 'proj_w': jax.random.normal(ks[3], (D, D), dtype=jnp.float32) * s, 'proj_b': jax.random.normal(ks[4], (D,), dtype=jnp.float32) * s}
    _L0_attn_in = _L0_attn_setup()

    def _L0_ffn_setup():
        import jax, jax.numpy as jnp
        import numpy as np
        D_IN, D_HID = (128, 512)

        def _ternary(key, shape):
            return jax.random.randint(key, shape, -1, 2).astype(jnp.float32)

        def _tlin(x, w, s):
            return jnp.einsum('bsi,oi->bso', x, w) * s
        key = jax.random.key(seed)
        ks = jax.random.split(key, 12)
        inv = lambda fan: 1.0 / np.sqrt(fan).astype(np.float32)
        return {'x': jax.random.normal(ks[0], (4, 256, D_IN), dtype=jnp.float32), 'w1_w': _ternary(ks[1], (D_HID, D_IN)), 'w1_s': jax.random.uniform(ks[2], (D_HID,), dtype=jnp.float32) * inv(D_IN), 'w2_w': _ternary(ks[3], (D_HID, D_IN)), 'w2_s': jax.random.uniform(ks[4], (D_HID,), dtype=jnp.float32) * inv(D_IN), 'h1_w': _ternary(ks[5], (D_HID, D_HID)), 'h1_s': jax.random.uniform(ks[6], (D_HID,), dtype=jnp.float32) * inv(D_HID), 'h2_w': _ternary(ks[7], (D_HID, D_HID)), 'h2_s': jax.random.uniform(ks[8], (D_HID,), dtype=jnp.float32) * inv(D_HID), 'w3_w': _ternary(ks[9], (D_IN, D_HID)), 'w3_s': jax.random.uniform(ks[10], (D_IN,), dtype=jnp.float32) * inv(D_HID)}
    _L0_ffn_in = _L0_ffn_setup()
    _d = {'L0_attn_x': _L0_attn_in['x'], 'L0_attn_qkv_w': _L0_attn_in['qkv_w'], 'L0_attn_qkv_b': _L0_attn_in['qkv_b'], 'L0_attn_proj_w': _L0_attn_in['proj_w'], 'L0_attn_proj_b': _L0_attn_in['proj_b'], 'L0_ffn_w1_w': _L0_ffn_in['w1_w'], 'L0_ffn_w1_s': _L0_ffn_in['w1_s'], 'L0_ffn_w2_w': _L0_ffn_in['w2_w'], 'L0_ffn_w2_s': _L0_ffn_in['w2_s'], 'L0_ffn_h1_w': _L0_ffn_in['h1_w'], 'L0_ffn_h1_s': _L0_ffn_in['h1_s'], 'L0_ffn_h2_w': _L0_ffn_in['h2_w'], 'L0_ffn_h2_s': _L0_ffn_in['h2_s'], 'L0_ffn_w3_w': _L0_ffn_in['w3_w'], 'L0_ffn_w3_s': _L0_ffn_in['w3_s']}
    _x0 = _d['L0_attn_x']
    _d['L0_attn_x'] = jax.random.normal(jax.random.fold_in(jax.random.key(seed), 1), (16, 512, 128), dtype=_x0.dtype)
    del _x0
    return _d

def reference(L0_attn_x, L0_attn_qkv_w, L0_attn_qkv_b, L0_attn_proj_w, L0_attn_proj_b, L0_ffn_w1_w, L0_ffn_w1_s, L0_ffn_w2_w, L0_ffn_w2_s, L0_ffn_h1_w, L0_ffn_h1_s, L0_ffn_h2_w, L0_ffn_h2_s, L0_ffn_w3_w, L0_ffn_w3_s):

    def _L0_attn_ref(x, qkv_w, qkv_b, proj_w, proj_b):
        import jax, jax.numpy as jnp
        import numpy as np
        B, N, D = (2, 256, 128)
        H = 16
        HD = D // H
        ROPE_BASE = 10000.0

        def _rotate_half(t):
            t = t.reshape(*t.shape[:-1], -1, 2)
            x1, x2 = (t[..., 0], t[..., 1])
            return jnp.stack((-x2, x1), axis=-1).reshape(*t.shape[:-2], -1)

        def _apply_rope(t, cos, sin):
            return t * cos + _rotate_half(t) * sin
        b, n, d = x.shape
        scale = HD ** (-0.5)
        qkv = x @ qkv_w.T + qkv_b
        qkv = qkv.reshape(b, n, 3, H, HD)
        qkv = jnp.transpose(qkv, (2, 0, 3, 1, 4))
        q, k, v = (qkv[0], qkv[1], qkv[2])
        inv_freq = 1.0 / ROPE_BASE ** (jnp.arange(0, HD, 2, dtype=jnp.float32) / HD)
        freqs = jnp.arange(n, dtype=jnp.float32)[:, None] * inv_freq[None, :]
        freqs = jnp.repeat(freqs, 2, axis=-1)
        cos, sin = (jnp.cos(freqs), jnp.sin(freqs))
        q = _apply_rope(q, cos, sin)
        k = _apply_rope(k, cos, sin)
        scores = jnp.einsum('bhid,bhjd->bhij', q, k) * scale
        causal = jnp.triu(jnp.ones((n, n), dtype=bool), k=1)
        scores = jnp.where(causal, -jnp.inf, scores)
        attn = jax.nn.softmax(scores, axis=-1)
        out = jnp.einsum('bhij,bhjd->bhid', attn, v)
        out = jnp.transpose(out, (0, 2, 1, 3)).reshape(b, n, d)
        return out @ proj_w.T + proj_b

    def _L0_ffn_ref(x, w1_w, w1_s, w2_w, w2_s, h1_w, h1_s, h2_w, h2_s, w3_w, w3_s):
        import jax, jax.numpy as jnp
        import numpy as np
        D_IN, D_HID = (128, 512)

        def _ternary(key, shape):
            return jax.random.randint(key, shape, -1, 2).astype(jnp.float32)

        def _tlin(x, w, s):
            return jnp.einsum('bsi,oi->bso', x, w) * s
        h = jax.nn.silu(_tlin(x, w1_w, w1_s)) * _tlin(x, w2_w, w2_s)
        h = jax.nn.gelu(_tlin(h, h1_w, h1_s), approximate=False)
        h = jax.nn.gelu(_tlin(h, h2_w, h2_s), approximate=False)
        return _tlin(h, w3_w, w3_s)
    x = L0_attn_x
    x = x + _layernorm(_L0_attn_ref(_layernorm(x, axis=-1), L0_attn_qkv_w, L0_attn_qkv_b, L0_attn_proj_w, L0_attn_proj_b), axis=-1)
    x = x + _layernorm(_L0_ffn_ref(_layernorm(x, axis=-1), L0_ffn_w1_w, L0_ffn_w1_s, L0_ffn_w2_w, L0_ffn_w2_s, L0_ffn_h1_w, L0_ffn_h1_s, L0_ffn_h2_w, L0_ffn_h2_s, L0_ffn_w3_w, L0_ffn_w3_s), axis=-1)
    return x

_drawn_inputs = setup_inputs


def setup_inputs(seed=0):
    import zlib

    import numpy as np

    out = dict(_drawn_inputs(seed))
    spreads = {}
    factors = {}
    for name, (base, spread) in spreads.items():
        noise = np.random.default_rng([zlib.crc32(name.encode()), seed]).standard_normal(out[name].shape)
        drawn = base * np.exp(spread * noise) if base else spread * noise
        out[name] = jnp.asarray(drawn.astype(out[name].dtype))
    for name, factor in factors.items():
        out[name] = (out[name] * factor).astype(out[name].dtype)
    return out
```

```python
from contextlib import ExitStack

import numpy as np

import concourse.bass as bass
from concourse import mybir

F32 = mybir.dt.float32
F32R = mybir.dt.float32r
ALU = mybir.AluOpType
ACT = mybir.ActivationFunctionType
AX_X = mybir.AxisListType.X

P = 128
BATCHES, TOKENS, D = 16, 512, 128
HEADS, HD = 16, 8
HIDDEN = 512
TILES = TOKENS // P
GROUPS, PER = 4, 4
ROWS = 32
SPLIT_ROWS = 3 * HD
SCORE_ROWS = SPLIT_ROWS + 2
KT = HIDDEN // P
EPS = 1e-5
SCALE = float(HD) ** -0.5
MASKED = -3.0e38
SLOTS = 3
UNITS = GROUPS * TILES
LAG = 2
PRING = 3
ROPE_BASE = 10000.0

W_COLS = {"w1": HIDDEN, "w2": HIDDEN, "h1": KT * HIDDEN, "h2": KT * HIDDEN, "w3": KT * D}
W_AT = {}
_at = 0
for _name, _n in W_COLS.items():
    W_AT[_name] = _at
    _at += _n
W_ALL = _at

F_ORDER = [("m3", 0), ("xn", 2), ("on", -1), ("proj", -1), ("m0", 1), ("v0", 2), ("v1", 2), ("v2", 2),
           ("v3", 2), ("m1", 1), ("q0", 2), ("k0", 2), ("m2", 1), ("q1", 2), ("k1", 2), ("q2", 2),
           ("k2", 2), ("q3", 2), ("k3", 2)]
FIRST_TURN, LAST_TURN = -2, BATCHES
LOOP_FROM, LOOPS = 1, 4


def in_range(n):
    return 0 <= n < BATCHES


def fills_before(k):
    return sum(in_range(t + d) for t in range(FIRST_TURN, k) for _, d in F_ORDER)


def positive(value):
    return max(value, 0) if isinstance(value, int) else value


class Turn:

    def __init__(self, j, c, looped):
        self.j, self.c, self.looped = j, c, looped

    def __add__(self, d):
        return Turn(self.j, self.c + d, self.looped)

    def exists(self):
        return self.looped or in_range(self.c)

    @property
    def n(self):
        return self.j * SLOTS + self.c if self.looped else self.c

    @property
    def slot(self):
        return self.c % SLOTS

    def count(self, per, more):
        n = self.c * per + more
        return self.j * (SLOTS * per) + n if self.looped else positive(n)

    def filled(self, name, more=1):
        n = fills_before(self.c)
        for x, d in F_ORDER:
            if x == name:
                break
            n += self.looped or in_range(self.c + d)
        n += more
        return self.j * (SLOTS * len(F_ORDER)) + n if self.looped else n


def turns(eng, body):
    for c in range(FIRST_TURN, LOOP_FROM):
        body(Turn(0, c, False))
    with eng.Fori(0, LOOPS) as j:
        for c in range(SLOTS):
            body(Turn(j, LOOP_FROM + c, True))
    for c in range(LOOP_FROM + SLOTS * LOOPS, LAST_TURN + 1):
        body(Turn(0, c, False))


def build(nc, x_in, qkv_w, proj_w, qkv_b, proj_b, ffn_w, hid_s, out_s, rope, out):
    x_tiles = x_in.rearrange("b (t p) d -> b p t d", p=P)
    out_tiles = out.rearrange("b (t p) d -> b p t d", p=P)
    scratch = nc.dram_tensor("x1_scratch", (BATCHES, P, TOKENS), F32, kind="Internal").ap()

    ctx = ExitStack()
    with ctx:
        def sb(name, shape, dt=F32):
            return ctx.enter_context(nc.sbuf_tensor(name, shape, dt))

        def psum(name, shape):
            return ctx.enter_context(nc.psum_tensor(name, shape, F32))

        def sem(name):
            return ctx.enter_context(nc.semaphore(name))

        bankE = psum("bankE", [P, 4, 512])
        bankS = psum("bankS", [P, 2, 512])
        bankB = psum("bankB", [P, 512])
        bankF = psum("bankF", [P, 512])

        wqkv = sb("wqkv", [P, 3 * D])
        wproj = sb("wproj", [P, D])
        qkvb = sb("qkvb", [P, 3 * D])
        projb = sb("projb", [P, D])
        ropes = sb("ropes", [P, 2 * TILES, 2 * HD])
        ident = sb("ident", [P, P])
        ident_r = sb("ident_r", [P, P], F32R)
        later = sb("later", [P, TOKENS])
        neg_half = sb("neg_half", [P, TILES])
        stage = sb("stage", [P, W_ALL])
        hids = sb("hids", [P, 4 * KT])
        half12 = sb("half12", [P, 2 * KT])
        outs_ = sb("outs_", [P, D])

        arena = sb("arena", [P, 2 * SLOTS * GROUPS * TOKENS], F32R)
        kT = arena[:, 0:SLOTS * GROUPS * TOKENS].rearrange("p (s g n) -> p s g n", s=SLOTS, g=GROUPS)
        qT = arena[:, SLOTS * GROUPS * TOKENS:].rearrange("p (s g n) -> p s g n", s=SLOTS, g=GROUPS)
        w_hi = arena[:, 0:W_ALL]
        w_lo = arena[:, W_ALL:2 * W_ALL]
        H_COLS = 2 * KT * TOKENS
        rows = sb("rows", [P, 3 * H_COLS + 2 * TOKENS], F32R)
        q_cols = TILES * HEADS * ROWS
        qrows = rows[:, 0:SLOTS * q_cols].rearrange("p (s t h r) -> p s t h r", s=SLOTS, t=TILES, h=HEADS)
        krows = rows[:, SLOTS * q_cols:(SLOTS + 1) * q_cols].rearrange("p (t h r) -> p t h r", t=TILES, h=HEADS)
        qrows_c = rows[:, 0:SLOTS * q_cols].rearrange("p (s t c) -> p s t c", s=SLOTS, t=TILES)
        krows_c = rows[:, SLOTS * q_cols:(SLOTS + 1) * q_cols].rearrange("p (t c) -> p t c", t=TILES)

        def hidden(i):
            v = rows[:, i * H_COLS:(i + 1) * H_COLS].rearrange("p (s k n) -> p s k n", s=2, k=KT)
            return v[:, 0], v[:, 1]

        (h0_hi, h0_lo), (h1_hi, h1_lo), (h2_hi, h2_lo) = hidden(0), hidden(1), hidden(2)
        xt_hi = rows[:, 3 * H_COLS:3 * H_COLS + TOKENS]
        xt_lo = rows[:, 3 * H_COLS + TOKENS:3 * H_COLS + 2 * TOKENS]

        x_ln = sb("x_ln", [P, TILES, D])
        x_res = sb("x_res", [P, TILES, D])
        v_sb = sb("v_sb", [P, SLOTS, TILES, HEADS, ROWS])
        probs = sb("probs", [P, PRING, PER, TOKENS])
        stats = sb("stats", [P, TILES, 6])
        meanvar = sb("meanvar", [P, TILES, 2])
        veps = sb("veps", [P, TILES])
        rstd = sb("rstd", [P, TILES])
        xn = sb("xn", [P, TILES, D])
        xnT = sb("xnT", [P, TOKENS])
        qk = sb("qk", [P, 2, TILES, D])
        rot = sb("rot", [P, 2, TILES, D])
        turned = sb("turned", [P, 2, TILES, D])
        rowmax = sb("rowmax", [P, TILES, HEADS])
        oT_rows = sb("oT_rows", [P, TOKENS])
        rden = sb("rden", [P, TILES, PER])
        o_tok = sb("o_tok", [P, TILES, D])
        oT = sb("oT", [P, TOKENS])
        y = turned[:, 0]
        stats_y = sb("stats_y", [P, TILES, 6])
        meanvar_y = sb("meanvar_y", [P, TILES, 2])
        veps_y = sb("veps_y", [P, TILES])
        rstd_y = sb("rstd_y", [P, TILES])
        x1 = sb("x1", [P, TILES, D])

        consts_in = sem("consts_in")
        ffn_in = sem("ffn_in")
        mask_step = sem("mask_step")
        pool_held = sem("pool_held")
        dve_held = sem("dve_held")
        consts_made = sem("consts_made")
        x_in = sem("x_in")
        x_res_in = sem("x_res_in")
        ln_step = sem("ln_step")
        var_ready = sem("var_ready")
        rstd_ready = sem("rstd_ready")
        xn_ready = sem("xn_ready")
        f_full = sem("f_full")
        f_empty = sem("f_empty")
        rope_step = sem("rope_step")
        hi_ready = sem("hi_ready")
        lo_ready = sem("lo_ready")
        s_full = sem("s_full")
        s_reduced = sem("s_reduced")
        max_split = sem("max_split")
        e_full = sem("e_full")
        exp_done = sem("exp_done")
        causal_done = sem("causal_done")
        pv_done = sem("pv_done")
        oT_rows_ready = sem("oT_rows_ready")
        o_turned = sem("o_turned")
        o_normed = sem("o_normed")
        y_step = sem("y_step")
        y_var = sem("y_var")
        y_rstd = sem("y_rstd")
        x1_ready = sem("x1_ready")
        x1_stored = sem("x1_stored")

        phase_a = ExitStack()
        block = phase_a.enter_context(nc.Block())

        @block.sync
        def _(sp):
            for dst, src in ((wqkv, qkv_w), (qkvb, qkv_b), (wproj, proj_w), (projb, proj_b)):
                sp.dma_start(dst[:], src).then_inc(consts_in, 16)
            sp.dma_start(ropes[:].rearrange("p t c -> p (t c)"), rope).then_inc(consts_in, 16)

            def turn(k):
                pre, fin = k + 3, k + -1
                if pre.exists():
                    sp.wait_ge(xn_ready, pre.count(1, 0))
                    sp.dma_start(x_ln[:], x_tiles[pre.n]).then_inc(x_in, 16)
                if fin.exists():
                    sp.wait_ge(x1_ready, fin.count(1, 0))
                    sp.dma_start(x_res[:], x_tiles[fin.n]).then_inc(x_res_in, 16)
                    sp.wait_ge(x1_ready, fin.count(1, 1))
                    sp.dma_start(scratch[fin.n], x1[:].rearrange("p t d -> p (t d)")).then_inc(x1_stored, 16)

            sp.dma_start(x_ln[:], x_tiles[0]).then_inc(x_in, 16)
            turn(Turn(0, -2, False))
            sp.dma_start(stage[:], ffn_w).then_inc(ffn_in, 16)
            sp.dma_start(hids[:], hid_s).then_inc(ffn_in, 16)
            sp.dma_start(outs_[:], out_s).then_inc(ffn_in, 16)
            for c in range(FIRST_TURN + 1, LOOP_FROM):
                turn(Turn(0, c, False))
            with sp.Fori(0, LOOPS) as j:
                for c in range(SLOTS):
                    turn(Turn(j, LOOP_FROM + c, True))
            for c in range(LOOP_FROM + SLOTS * LOOPS, LAST_TURN + 1):
                turn(Turn(0, c, False))
            sp.wait_ge(x1_stored, 16 * BATCHES)

        @block.gpsimd
        def _(pool):
            nc.gpsimd.memset(ident[:], 0.0)
            nc.gpsimd.memset(ident_r[:].bitcast(F32), 0.0)
            nc.gpsimd.memset(later[:], 0.0)
            nc.gpsimd.memset(neg_half[:], -0.5).then_inc(mask_step, 1)
            pool.wait_ge(mask_step, 1)
            for t in (ident[:], ident_r[:]):
                nc.gpsimd.affine_select(out=t, in_=t.bitcast(F32), compare_op=ALU.not_equal, fill=1.0, base=0,
                                        pattern=[[-1, P]], channel_multiplier=1)
            nc.gpsimd.affine_select(out=later[:, TOKENS - P:], in_=later[:, TOKENS - P:], compare_op=ALU.is_ge,
                                    fill=MASKED, base=0, pattern=[[-1, P]],
                                    channel_multiplier=1).then_inc(consts_made, 1)
            pool.wait_ge(consts_in, 16 * 5)
            pool.wait_ge(consts_made, 1)
            cos = ropes[:, :, 0:HD].unsqueeze(2).to_broadcast([P, 2 * TILES, HEADS, HD])
            sin_even = ropes[:, :, HD:HD + HD // 2].unsqueeze(2).to_broadcast([P, 2 * TILES, HEADS, HD // 2])
            sin_odd = ropes[:, :, HD + HD // 2:].unsqueeze(2).to_broadcast([P, 2 * TILES, HEADS, HD // 2])

            def heads(t):
                return t[:].rearrange("p a t (h d) -> p (a t) h d", h=HEADS)

            def even(t):
                return heads(t)[:, :, :, 0:HD:2]

            def odd(t):
                return heads(t)[:, :, :, 1:HD:2]

            def turn(k):
                pre, att, fin = k + 2, k, k + -1
                for u in range(UNITS):
                    if u == 0 and pre.exists():
                        pool.wait_ge(var_ready, pre.count(1, 1))
                        nc.gpsimd.tensor_tensor(rstd[:], veps[:], neg_half[:], ALU.pow).then_inc(rstd_ready, 1)
                    if u == 5 and fin.exists():
                        pool.wait_ge(y_var, fin.count(1, 1))
                        nc.gpsimd.tensor_tensor(rstd_y[:], veps_y[:], neg_half[:], ALU.pow).then_inc(y_rstd, 1)
                    if u == 9 and pre.exists():
                        pool.wait_ge(f_empty, k.filled("v3"))
                        nc.gpsimd.tensor_tensor(heads(rot), heads(qk), cos, ALU.mult).then_inc(rope_step, 1)
                        nc.gpsimd.tensor_tensor(even(turned), odd(qk), sin_even, ALU.mult).then_inc(rope_step, 1)
                    if u == 10 and pre.exists():
                        nc.gpsimd.tensor_tensor(odd(turned), even(qk), sin_odd, ALU.mult).then_inc(rope_step, 1)
                        pool.wait_ge(rope_step, pre.count(4, 3))
                        nc.gpsimd.tensor_tensor(rot[:].rearrange("p a t d -> p (a t d)"),
                                                rot[:].rearrange("p a t d -> p (a t d)"),
                                                turned[:].rearrange("p a t d -> p (a t d)"),
                                                ALU.add).then_inc(rope_step, 1)
                    if att.exists():
                        pool.wait_ge(exp_done, att.count(2 * UNITS, 2 * u + 2))
                        pool.sem_inc(pool_held, 1)
                        diag = probs[:, (UNITS * att.c + u) % PRING, :, 0:P]
                        nc.gpsimd.affine_select(out=diag, in_=diag, compare_op=ALU.is_ge, fill=0.0, base=0,
                                                pattern=[[0, PER], [1, P]],
                                                channel_multiplier=-1).then_inc(causal_done, 1)

            turns(pool, turn)

        @block.tensor
        def _(pe):
            pe.wait_ge(consts_in, 16 * 5)
            pe.wait_ge(consts_made, 1)

            def f_free(k, name):
                pe.wait_ge(f_empty, k.filled(name, 0))

            def transposes(k, name, source):
                f_free(k, name)
                for t in range(TILES):
                    rows_in, dst = source(t), bankF[:, t * P:(t + 1) * P]
                    if rows_in.dtype == F32R:
                        last = nc.tensor.transpose(dst.bitcast(F32R), rows_in, ident_r[:])
                    else:
                        last = nc.tensor.transpose(dst, rows_in, ident[:])
                last.then_inc(f_full, 1)

            def turn(k):
                pre, mx, att, fin = k + 2, k + 1, k, k + -1

                def requery(b, g):
                    if b.exists():
                        pe.wait_ge(max_split, b.count(2 * GROUPS, 2 * g + 2))
                        transposes(k, f"m{g}", lambda t: qrows_c[:, b.slot, t, g * P:(g + 1) * P])

                def head_rows(name, g):
                    if pre.exists():
                        pe.wait_ge(hi_ready, pre.count(2, 2))
                        pe.wait_ge(lo_ready, pre.count(2, 2))
                        if name == "q":
                            transposes(k, f"q{g}", lambda t: qrows_c[:, pre.slot, t, g * P:(g + 1) * P])
                        else:
                            transposes(k, f"k{g}", lambda t: krows_c[:, t, g * P:(g + 1) * P])

                def exp_scores(u, pair):
                    if not att.exists():
                        return
                    g, kt = u // TILES, u % TILES
                    if kt == 0 and pair == 0:
                        pe.wait_ge(f_empty, (k if g == 3 else k + -1).filled(f"m{g}"))
                    pe.wait_ge(exp_done, att.count(2 * UNITS, 2 * u + pair - 1))
                    for i in range(2):
                        r = ROWS * (2 * pair + i)
                        last = nc.tensor.matmul(bankE[:, 2 * pair + i, 0:TOKENS - kt * P],
                                                kT[r:r + SCORE_ROWS, att.slot, g, kt * P:(kt + 1) * P],
                                                qT[r:r + SCORE_ROWS, att.slot, g, kt * P:TOKENS],
                                                start=True, stop=True)
                    last.then_inc(e_full, 1)

                def max_scores(u, j):
                    if not mx.exists():
                        return
                    g, qt = u // TILES, TILES - 1 - u % TILES
                    if u % TILES == 0 and j == 0:
                        pe.wait_ge(f_empty, (k + -1).filled(f"k{g}"))
                    pe.wait_ge(s_reduced, mx.count(UNITS * PER, PER * u + j - 1))
                    nk = (qt + 1) * P
                    nc.tensor.matmul(bankS[:, j % 2, 0:nk],
                                     qT[ROWS * j:ROWS * j + SPLIT_ROWS, mx.slot, g, qt * P:nk],
                                     kT[ROWS * j:ROWS * j + SPLIT_ROWS, mx.slot, g, 0:nk],
                                     start=True, stop=True).then_inc(s_full, 1)

                def p_v(b, u):
                    if not b.exists():
                        return
                    g, kt = u // TILES, u % TILES
                    pe.wait_ge(causal_done, b.count(UNITS, u + 1))
                    if kt == 0:
                        pe.wait_ge(o_normed, b.count(2 * GROUPS, 2 * g))
                    for j in range(PER):
                        last = nc.tensor.matmul(bankB[ROWS * j:ROWS * (j + 1), kt * P:TOKENS],
                                                v_sb[:, b.slot, kt, g * PER + j, :],
                                                probs[:, (UNITS * b.c + u) % PRING, j, 0:TOKENS - kt * P],
                                                start=(kt == 0), stop=(kt == TILES - 1))
                    last.then_inc(pv_done, 1)

                def turn_o(b, g):
                    if b.exists():
                        pe.wait_ge(oT_rows_ready, b.count(GROUPS, g + 1))
                        for t in range(TILES):
                            last = nc.tensor.transpose(bankB[:, t * P:(t + 1) * P],
                                                       oT_rows[:, t * P:(t + 1) * P], ident[:])
                        last.then_inc(o_turned, 1)

                for u in range(UNITS):
                    if u in (1, 5, 9, 13):
                        g = (u - 5) // TILES
                        requery(att if u == 1 else mx, g % GROUPS)
                    exp_scores(u, 0)
                    if u % TILES == 2:
                        turn_o(fin if u == 2 else att, (u - 6) // TILES % GROUPS)
                    if u == 2 and pre.exists():
                        pe.wait_ge(xn_ready, pre.count(1, 1))
                        transposes(k, "xn", lambda t: xn[:, t, :])
                    if u == 3 and fin.exists():
                        pe.wait_ge(o_normed, fin.count(2 * GROUPS, 2 * GROUPS))
                        transposes(k, "on", lambda t: o_tok[:, t, :])
                    if u >= 12:
                        head_rows("q", u - 12)
                    max_scores(u, 0)
                    max_scores(u, 1)
                    exp_scores(u, 1)
                    max_scores(u, 2)
                    max_scores(u, 3)
                    if u == 4 and fin.exists():
                        f_free(k, "proj")
                        for t in range(TILES):
                            last = nc.tensor.matmul(bankF[:, t * P:(t + 1) * P], oT[:, t * P:(t + 1) * P],
                                                    wproj[:], start=True, stop=True)
                        last.then_inc(f_full, 1)
                    if 5 <= u < 9 and pre.exists():
                        t = u - 5
                        f_free(k, f"v{t}")
                        nc.tensor.matmul(bankF[:, 0:3 * D], xnT[:, t * P:(t + 1) * P], wqkv[:],
                                         start=True, stop=True).then_inc(f_full, 1)
                    if u >= 12:
                        head_rows("k", u - 12)
                    p_v(att if u >= LAG else fin, (u - LAG) % UNITS)

            turns(pe, turn)

        @block.scalar
        def _(act):
            def leave_f(k, name, dst):
                act.wait_ge(f_full, k.filled(name))
                nc.scalar.activation(dst, bankF[:], ACT.Copy).then_inc(f_empty, 1)

            def turn(k):
                pre, mx, att, fin = k + 2, k + 1, k, k + -1

                def exp_pair(u, pair):
                    if not att.exists():
                        return
                    nq = TOKENS - u % TILES * P
                    act.wait_ge(e_full, att.count(2 * UNITS, 2 * u + pair + 1))
                    act.wait_ge(pv_done, att.count(UNITS, u - PRING + 1))
                    nc.scalar.activation(probs[:, (UNITS * att.c + u) % PRING, 2 * pair:2 * pair + 2, 0:nq],
                                         bankE[:, 2 * pair:2 * pair + 2, 0:nq], ACT.Exp,
                                         scale=SCALE).then_inc(exp_done, 1)

                for u in range(UNITS):
                    done = fin if u == 2 else att
                    if u % TILES == 2 and done.exists():
                        g = (u - 6) // TILES % GROUPS
                        act.wait_ge(pv_done, done.count(UNITS, TILES * g + TILES))
                        nc.scalar.activation(oT_rows[:], bankB[:], ACT.Copy).then_inc(oT_rows_ready, 1)
                    exp_pair(u, 0)
                    if u in (1, 5, 9, 13):
                        b, g = (att if u == 1 else mx), (u - 5) // TILES % GROUPS
                        if b.exists():
                            leave_f(k, f"m{g}", qT[:, b.slot, g, :])
                    if u == 2 and pre.exists():
                        leave_f(k, "xn", xnT[:])
                    if u == 3 and fin.exists():
                        leave_f(k, "on", oT[:])
                    if u == 11 and pre.exists():
                        act.wait_ge(rope_step, pre.count(4, 4))
                        q_src, k_src = (rot[:, i].rearrange("p t (h d) -> p (t h) d", h=HEADS).unsqueeze(2)
                                        .to_broadcast([P, TILES * HEADS, 2, HD]) for i in range(2))
                        q_dst = qrows[:, pre.slot, :, :, 0:2 * HD].rearrange("p t h (a d) -> p (t h) a d", a=2)
                        k_dst = krows[:, :, :, 0:4 * HD].rearrange("p t h (a d) -> p (t h) a d", a=4)[:, :, 0:3:2, :]
                        nc.scalar.activation(q_dst, q_src, ACT.Copy).then_inc(hi_ready, 1)
                        nc.scalar.activation(k_dst, k_src, ACT.Copy).then_inc(hi_ready, 1)
                    if u >= 12 and pre.exists():
                        leave_f(k, f"q{u - 12}", qT[:, pre.slot, u - 12, :])
                    exp_pair(u, 1)
                    if u >= 12 and pre.exists():
                        leave_f(k, f"k{u - 12}", kT[:, pre.slot, u - 12, :])

            act.wait_ge(ln_step, 1)
            turns(act, turn)

        @block.vector
        def _(dve):
            nc.vector.memset(rows[:, 0:(SLOTS + 1) * q_cols].bitcast(F32), 0.0)
            nc.vector.memset(v_sb[:], 0.0).then_inc(consts_made, 1)
            dve.wait_ge(consts_made, 2)
            nc.vector.memset(v_sb[:].rearrange("p s t h r -> p (s t h) r")[:, :, HD:HD + 1], 1.0)
            nc.vector.memset(krows[:].rearrange("p t h r -> p (t h) r")[:, :, SPLIT_ROWS:SCORE_ROWS].bitcast(F32),
                             1.0).then_inc(ln_step, 1)
            dve.wait_ge(ln_step, 1)
            dve.wait_ge(consts_in, 16 * 5)

            def turn(k):
                pre, mx, att, fin = k + 2, k + 1, k, k + -1

                def split_max(b, g):
                    if not b.exists():
                        return
                    src = rowmax[:, :, PER * g:PER * (g + 1)]
                    at = qrows[:, b.slot, :, PER * g:PER * (g + 1), :]
                    dve.wait_ge(s_reduced, b.count(UNITS * PER, TILES * PER * (g + 1)))
                    nc.vector.tensor_scalar(at[:, :, :, SPLIT_ROWS], src, -1.0, None, ALU.mult).then_inc(max_split, 1)
                    dve.wait_ge(max_split, b.count(2 * GROUPS, 2 * g + 1))
                    nc.vector.scalar_tensor_tensor(out=at[:, :, :, SPLIT_ROWS + 1], in0=src, scalar=-1.0,
                                                   in1=at[:, :, :, SPLIT_ROWS].bitcast(F32), op0=ALU.mult,
                                                   op1=ALU.subtract).then_inc(max_split, 1)

                def norm_o(b, g):
                    if not b.exists():
                        return
                    dve.wait_ge(o_turned, b.count(GROUPS, g + 1))
                    turned_o = bankB[:].rearrange("p (t j r) -> p t j r", t=TILES, j=PER)
                    nc.vector.reciprocal(rden[:], turned_o[:, :, :, HD]).then_inc(o_normed, 1)
                    dve.wait_ge(o_normed, b.count(2 * GROUPS, 2 * g + 1))
                    nc.vector.tensor_tensor(
                        o_tok[:, :, g * PER * HD:(g + 1) * PER * HD].rearrange("p t (j d) -> p t j d", j=PER),
                        turned_o[:, :, :, 0:HD],
                        rden[:].unsqueeze(3).to_broadcast([P, TILES, PER, HD]), ALU.mult).then_inc(o_normed, 1)

                for u in range(UNITS):
                    if u % TILES == 0:
                        split_max(att if u == 0 else mx, (u // TILES - 1) % GROUPS)
                    if u == 0 and pre.exists():
                        dve.wait_ge(x_in, pre.count(16, 16))
                        for t in range(TILES):
                            last = nc.vector.bn_stats(stats[:, t, :], x_ln[:, t, :])
                        last.then_inc(ln_step, 1)
                        dve.wait_ge(ln_step, pre.count(2, 2))
                        dve.sem_inc(dve_held, 1)
                        for t in range(TILES):
                            last = nc.vector.bn_aggr(meanvar[:, t, :], stats[:, t, :])
                        last.then_inc(ln_step, 1)
                        dve.wait_ge(ln_step, pre.count(2, 3))
                        nc.vector.tensor_scalar(veps[:], meanvar[:, :, 1], EPS, None, ALU.add).then_inc(var_ready, 1)
                    if u == 1 and pre.exists():
                        dve.wait_ge(rstd_ready, pre.count(1, 1))
                        for t in range(TILES):
                            last = nc.vector.tensor_scalar(xn[:, t, :], x_ln[:, t, :], meanvar[:, t, 0:1],
                                                           rstd[:, t:t + 1], ALU.subtract, ALU.mult)
                        last.then_inc(xn_ready, 1)
                    if u == 5 and fin.exists():
                        dve.wait_ge(f_full, k.filled("proj"))
                        nc.vector.tensor_tensor(y, bankF[:].rearrange("p (t d) -> p t d", t=TILES),
                                                projb[:].unsqueeze(1).to_broadcast([P, TILES, D]),
                                                ALU.add).then_inc(f_empty, 1)
                        dve.wait_ge(f_empty, k.filled("proj"))
                        for t in range(TILES):
                            last = nc.vector.bn_stats(stats_y[:, t, :], y[:, t, :])
                        last.then_inc(y_step, 1)
                        dve.wait_ge(y_step, fin.count(3, 1))
                        dve.sem_inc(dve_held, 1)
                        for t in range(TILES):
                            last = nc.vector.bn_aggr(meanvar_y[:, t, :], stats_y[:, t, :])
                        last.then_inc(y_step, 1)
                        dve.wait_ge(y_step, fin.count(3, 2))
                        nc.vector.tensor_scalar(veps_y[:], meanvar_y[:, :, 1], EPS, None, ALU.add).then_inc(y_var, 1)
                    if 6 <= u < 10 and pre.exists():
                        t = u - 6
                        dve.wait_ge(f_full, k.filled(f"v{t}"))
                        nc.vector.tensor_tensor(qk[:, :, t, :], bankF[:, 0:2 * D].rearrange("p (a d) -> p a d", a=2),
                                                qkvb[:, 0:2 * D].rearrange("p (a d) -> p a d", a=2), ALU.add)
                        nc.vector.tensor_tensor(v_sb[:, pre.slot, t, :, 0:HD],
                                                bankF[:, 2 * D:3 * D].rearrange("p (h d) -> p h d", h=HEADS),
                                                qkvb[:, 2 * D:3 * D].rearrange("p (h d) -> p h d", h=HEADS),
                                                ALU.add).then_inc(f_empty, 1)
                    if u % TILES == 2:
                        norm_o(fin if u == 2 else att, (u - 6) // TILES % GROUPS)
                    if u == 7 and fin.exists():
                        dve.wait_ge(y_rstd, fin.count(1, 1))
                        for t in range(TILES):
                            last = nc.vector.tensor_scalar(y[:, t, :], y[:, t, :], meanvar_y[:, t, 0:1],
                                                           rstd_y[:, t:t + 1], ALU.subtract, ALU.mult)
                        last.then_inc(y_step, 1)
                        dve.wait_ge(y_step, fin.count(3, 3))
                        dve.wait_ge(x1_stored, fin.count(16, 0))
                        dve.wait_ge(x_res_in, fin.count(16, 16))
                        nc.vector.tensor_tensor(x1[:], y, x_res[:], ALU.add).then_inc(x1_ready, 1)
                    if u == 11 and pre.exists():
                        dve.wait_ge(hi_ready, pre.count(2, 2))
                        q_src, k_src = (rot[:, i].rearrange("p t (h d) -> p (t h) d", h=HEADS) for i in range(2))
                        q_at = qrows[:, pre.slot].rearrange("p t h r -> p (t h) r")
                        k_at = krows[:].rearrange("p t h r -> p (t h) r")
                        nc.vector.tensor_tensor(q_at[:, :, 2 * HD:3 * HD], q_src, q_at[:, :, 0:HD].bitcast(F32),
                                                ALU.subtract).then_inc(lo_ready, 1)
                        nc.vector.tensor_tensor(k_at[:, :, HD:2 * HD], k_src, k_at[:, :, 0:HD].bitcast(F32),
                                                ALU.subtract).then_inc(lo_ready, 1)
                    if mx.exists():
                        g, qt = u // TILES, TILES - 1 - u % TILES
                        for j in range(PER):
                            dve.wait_ge(s_full, mx.count(UNITS * PER, PER * u + j + 1))
                            dve.sem_inc(dve_held, 1)
                            score = bankS[:, j % 2, 0:(qt + 1) * P]
                            nc.vector.tensor_tensor_reduce(score, score, later[:, (TILES - 1 - qt) * P:], 1.0, MASKED,
                                                           ALU.add, ALU.max,
                                                           rowmax[:, qt, PER * g + j:PER * g + j + 1]
                                                           ).then_inc(s_reduced, 1)

            turns(dve, turn)

        phase_a.close()
        w_hi_ready = sem("w_hi_ready")
        w_lo_ready = sem("w_lo_ready")
        x1_in = sem("x1_in")
        res_in = sem("res_in")
        b_step = sem("b_step")
        b_var = sem("b_var")
        b_rstd = sem("b_rstd")
        b_xn = sem("b_xn")
        xt_full = sem("xt_full")
        xt_hi_ready = sem("xt_hi_ready")
        xt_lo_ready = sem("xt_lo_ready")
        au_full = sem("au_full")
        tanh_done = sem("tanh_done")
        gate_done = sem("gate_done")
        h0_done = sem("h0_done")
        h0_hi_ready = sem("h0_hi_ready")
        h0_lo_ready = sem("h0_lo_ready")
        layer_full = [sem("h1_full"), sem("h2_full")]
        gelu_done = [sem("h1_gelu"), sem("h2_gelu")]
        layer_lo = [sem("h1_lo_ready"), sem("h2_lo_ready")]
        w3_full = sem("w3_full")
        w3_empty = sem("w3_empty")
        c_step = sem("c_step")
        c_var = sem("c_var")
        c_rstd = sem("c_rstd")
        out_ready = sem("out_ready")
        out_stored = sem("out_stored")

        ffn_x = qk[:, 0]
        ffn_res = qk[:, 1]
        th = probs[:, 2, 0:2]
        gate = probs[:, 2, 2:4]
        h0_f = probs[:, 0]
        act_f = probs[:, 1]
        out_sb = x1

        def chunks(eng, body):
            for i in range(-2, 1):
                body(i, False)
            with eng.Fori(1, BATCHES - 3) as i:
                body(i, True)
            for i in range(BATCHES - 3, BATCHES + 1):
                body(i, False)

        def live(c, looped):
            return looped or in_range(c)

        def split3(pe, bank, w0, k_hi, k_lo, first, last):
            n = w0.stop - w0.start
            nc.tensor.matmul(bank, w_hi[:, w0], k_hi, start=first, stop=False)
            nc.tensor.matmul(bank, w_hi[:, w0], k_lo, start=False, stop=False)
            return nc.tensor.matmul(bank, w_lo[:, w0], k_hi, start=False, stop=last)

        block_b = ctx.enter_context(nc.Block())

        @block_b.sync
        def _(sp):
            def turn(i, looped):
                if live(i + 3, looped):
                    sp.wait_ge(b_xn, i + 3)
                    sp.dma_start(ffn_x.rearrange("p t d -> p (t d)"), scratch[i + 3]).then_inc(x1_in, 16)
                if live(i, looped):
                    sp.wait_ge(out_ready, i)
                    sp.dma_start(ffn_res.rearrange("p t d -> p (t d)"), scratch[i]).then_inc(res_in, 16)
                if live(i - 1, looped):
                    sp.wait_ge(out_ready, i)
                    sp.dma_start(out_tiles[i - 1], out_sb[:]).then_inc(out_stored, 16)

            sp.dma_start(ffn_x.rearrange("p t d -> p (t d)"), scratch[0]).then_inc(x1_in, 16)
            chunks(sp, turn)
            sp.wait_ge(out_stored, 16 * BATCHES)

        @block_b.gpsimd
        def _(pool):
            def turn(i, looped):
                if live(i + 2, looped):
                    pool.wait_ge(b_var, i + 3)
                    nc.gpsimd.tensor_tensor(rstd[:], veps[:], neg_half[:], ALU.pow).then_inc(b_rstd, 1)
                if live(i - 1, looped):
                    pool.wait_ge(c_var, i)
                    nc.gpsimd.tensor_tensor(rstd_y[:], veps_y[:], neg_half[:], ALU.pow).then_inc(c_rstd, 1)

            chunks(pool, turn)

        @block_b.tensor
        def _(pe):
            pe.wait_ge(w_hi_ready, 2)
            pe.wait_ge(w_lo_ready, 2)

            def layer(i, number, name, src_hi, src_lo, ready):
                for o in range(KT):
                    if o < 2:
                        pe.wait_ge(gelu_done[1 - number], positive((i - 1 + number) * KT + o + 3))
                    else:
                        pe.wait_ge(gelu_done[number], i * KT + o - 1)
                    for k in range(KT):
                        if o == 0:
                            pe.wait_ge(ready, i * KT + (k + 1))
                        at = W_AT[name] + k * HIDDEN + o * P
                        last = split3(pe, bankS[:, o % 2, :], slice(at, at + P), src_hi[:, k, :], src_lo[:, k, :],
                                      k == 0, k == KT - 1)
                    last.then_inc(layer_full[number], 1)

            def turn(i, looped):
                nxt, cur, prv = live(i + 1, looped), live(i, looped), live(i - 1, looped)
                if nxt:
                    pe.wait_ge(b_xn, i + 2)
                    for t in range(TILES):
                        last = nc.tensor.transpose(bankF[:, t * P:(t + 1) * P], xn[:, t, :], ident[:])
                    last.then_inc(xt_full, 1)
                if cur:
                    layer(i, 0, "h1", h0_hi, h0_lo, h0_lo_ready)
                if prv:
                    pe.wait_ge(w3_empty, i - 1)
                    pe.wait_ge(layer_lo[1], i * KT)
                    for t in range(TILES):
                        for k in range(KT):
                            at = W_AT["w3"] + k * D
                            h_at = slice(t * P, (t + 1) * P)
                            for n, (h, w) in enumerate(((h2_hi, w_hi), (h2_hi, w_lo), (h2_lo, w_hi))):
                                last = nc.tensor.matmul(bankB[:, h_at], h[:, k, h_at], w[:, at:at + D],
                                                        start=(k == 0 and n == 0), stop=(k == KT - 1 and n == 2))
                    last.then_inc(w3_full, 1)
                if nxt:
                    pe.wait_ge(xt_hi_ready, i + 2)
                    pe.wait_ge(xt_lo_ready, i + 2)
                    for o in range(KT):
                        pe.wait_ge(h0_done, positive((i + 1) * KT + o - 1))
                        for half, name in ((0, "w1"), (2, "w2")):
                            at = W_AT[name] + o * P
                            last = split3(pe, bankE[:, half + o % 2, :], slice(at, at + P), xt_hi, xt_lo, True, True)
                        last.then_inc(au_full, 1)
                if cur:
                    layer(i, 1, "h2", h1_hi, h1_lo, layer_lo[0])

            chunks(pe, turn)

        @block_b.scalar
        def _(act):
            act.wait_ge(ffn_in, 16 * 3)
            for n in range(2):
                half = slice(n * W_ALL // 2, (n + 1) * W_ALL // 2)
                nc.scalar.activation(w_hi[:, half], stage[:, half], ACT.Copy).then_inc(w_hi_ready, 1)
            act.wait_ge(b_step, 2)

            def layer(i, number, hi, read_by, times):
                for o in range(KT):
                    act.wait_ge(layer_full[number], i * KT + (o + 1))
                    if o == 0:
                        act.wait_ge(read_by, times)
                    scale = hids[:, (2 + number) * KT + o:(2 + number) * KT + o + 1]
                    nc.scalar.activation(hi[:, o, :], bankS[:, o % 2, :], ACT.Gelu, scale=scale)
                    if o < 2:
                        act.wait_ge(layer_lo[1 - number], positive((i - 1 + number) * KT + o + 3))
                    else:
                        act.wait_ge(layer_lo[number], i * KT + o - 1)
                    nc.scalar.activation(act_f[:, o % 2, :], bankS[:, o % 2, :], ACT.Gelu,
                                         scale=scale).then_inc(gelu_done[number], 1)

            def turn(i, looped):
                nxt, cur, prv = live(i + 1, looped), live(i, looped), live(i - 1, looped)
                if nxt:
                    act.wait_ge(xt_full, i + 2)
                    nc.scalar.activation(xt_hi, bankF[:], ACT.Copy).then_inc(xt_hi_ready, 1)
                if cur:
                    layer(i, 0, h1_hi, layer_full[1], i * KT)
                if nxt:
                    def h0_high(o):
                        act.wait_ge(h0_done, (i + 1) * KT + (o + 1))
                        nc.scalar.activation(h0_hi[:, o, :], h0_f[:, o, :], ACT.Copy).then_inc(h0_hi_ready, 1)

                    for o in range(KT):
                        act.wait_ge(au_full, (i + 1) * KT + (o + 1))
                        act.wait_ge(gate_done, positive((i + 1) * KT + o - 1))
                        nc.scalar.activation(th[:, o % 2, :], bankE[:, o % 2, :], ACT.Tanh,
                                             scale=half12[:, o:o + 1]).then_inc(tanh_done, 1)
                        if o == 0 and cur:
                            act.wait_ge(layer_full[0], (i + 1) * KT)
                        if o >= 1:
                            h0_high(o - 1)
                    h0_high(KT - 1)
                if cur:
                    layer(i, 1, h2_hi, w3_full, i)

            chunks(act, turn)

        @block_b.vector
        def _(dve):
            dve.wait_ge(ffn_in, 16 * 3)
            nc.vector.tensor_scalar(half12[:, 0:KT], hids[:, 0:KT], 0.5, None, ALU.mult).then_inc(b_step, 1)
            dve.wait_ge(b_step, 1)
            nc.vector.tensor_tensor(half12[:, KT:2 * KT], half12[:, 0:KT], hids[:, KT:2 * KT],
                                    ALU.mult).then_inc(b_step, 1)
            for n in range(2):
                half = slice(n * W_ALL // 2, (n + 1) * W_ALL // 2)
                dve.wait_ge(w_hi_ready, n + 1)
                nc.vector.tensor_tensor(w_lo[:, half], stage[:, half], w_hi[:, half].bitcast(F32),
                                        ALU.subtract).then_inc(w_lo_ready, 1)

            def layer_low(i, number, hi, lo):
                for o in range(KT):
                    dve.wait_ge(gelu_done[number], i * KT + (o + 1))
                    nc.vector.tensor_tensor(lo[:, o, :], act_f[:, o % 2, :], hi[:, o, :].bitcast(F32),
                                            ALU.subtract).then_inc(layer_lo[number], 1)

            def turn(i, looped):
                aft, nxt, cur, prv = (live(i + d, looped) for d in (2, 1, 0, -1))
                if nxt:
                    dve.wait_ge(xt_hi_ready, i + 2)
                    nc.vector.tensor_tensor(xt_lo, bankF[:], xt_hi.bitcast(F32), ALU.subtract).then_inc(xt_lo_ready, 1)
                if aft:
                    dve.wait_ge(x1_in, (i + 3) * 16)
                    for t in range(TILES):
                        last = nc.vector.bn_stats(stats[:, t, :], ffn_x[:, t, :])
                    last.then_inc(b_step, 1)
                    dve.wait_ge(b_step, (i + 2) * 2 + 3)
                    dve.sem_inc(dve_held, 1)
                    for t in range(TILES):
                        last = nc.vector.bn_aggr(meanvar[:, t, :], stats[:, t, :])
                    last.then_inc(b_step, 1)
                    dve.wait_ge(b_step, (i + 2) * 2 + 4)
                    nc.vector.tensor_scalar(veps[:], meanvar[:, :, 1], EPS, None, ALU.add).then_inc(b_var, 1)
                if cur:
                    layer_low(i, 0, h1_hi, h1_lo)
                if aft:
                    dve.wait_ge(b_rstd, i + 3)
                    for t in range(TILES):
                        last = nc.vector.tensor_scalar(xn[:, t, :], ffn_x[:, t, :], meanvar[:, t, 0:1],
                                                       rstd[:, t:t + 1], ALU.subtract, ALU.mult)
                    last.then_inc(b_xn, 1)
                if nxt:
                    for o in range(KT):
                        dve.wait_ge(tanh_done, (i + 1) * KT + (o + 1))
                        nc.vector.scalar_tensor_tensor(out=gate[:, o % 2, :], in0=th[:, o % 2, :], scalar=1.0,
                                                       in1=bankE[:, o % 2, :], op0=ALU.add,
                                                       op1=ALU.mult).then_inc(gate_done, 1)
                        dve.wait_ge(gate_done, (i + 1) * KT + (o + 1))
                        nc.vector.scalar_tensor_tensor(out=h0_f[:, o, :], in0=bankE[:, 2 + o % 2, :],
                                                       scalar=half12[:, KT + o:KT + o + 1],
                                                       in1=gate[:, o % 2, :], op0=ALU.mult,
                                                       op1=ALU.mult).then_inc(h0_done, 1)
                    for o in range(KT):
                        dve.wait_ge(h0_hi_ready, (i + 1) * KT + (o + 1))
                        nc.vector.tensor_tensor(h0_lo[:, o, :], h0_f[:, o, :], h0_hi[:, o, :].bitcast(F32),
                                                ALU.subtract).then_inc(h0_lo_ready, 1)
                if prv:
                    dve.wait_ge(out_ready, i - 1)
                    dve.wait_ge(w3_full, i)
                    nc.vector.tensor_tensor(y, bankB[:].rearrange("p (t d) -> p t d", t=TILES),
                                            outs_[:].unsqueeze(1).to_broadcast([P, TILES, D]),
                                            ALU.mult).then_inc(w3_empty, 1)
                    dve.wait_ge(w3_empty, i)
                    for t in range(TILES):
                        last = nc.vector.bn_stats(stats_y[:, t, :], y[:, t, :])
                    last.then_inc(c_step, 1)
                    dve.wait_ge(c_step, (i - 1) * 3 + 1)
                    dve.sem_inc(dve_held, 1)
                    for t in range(TILES):
                        last = nc.vector.bn_aggr(meanvar_y[:, t, :], stats_y[:, t, :])
                    last.then_inc(c_step, 1)
                    dve.wait_ge(c_step, (i - 1) * 3 + 2)
                    nc.vector.tensor_scalar(veps_y[:], meanvar_y[:, :, 1], EPS, None, ALU.add).then_inc(c_var, 1)
                if cur:
                    layer_low(i, 1, h2_hi, h2_lo)
                if prv:
                    dve.wait_ge(c_rstd, i)
                    for t in range(TILES):
                        last = nc.vector.tensor_scalar(y[:, t, :], y[:, t, :], meanvar_y[:, t, 0:1],
                                                       rstd_y[:, t:t + 1], ALU.subtract, ALU.mult)
                    last.then_inc(c_step, 1)
                    dve.wait_ge(c_step, (i - 1) * 3 + 3)
                    dve.wait_ge(res_in, i * 16)
                    dve.wait_ge(out_stored, (i - 1) * 16)
                    nc.vector.tensor_tensor(out_sb[:], y, ffn_res, ALU.add).then_inc(out_ready, 1)

            chunks(dve, turn)


def rope_table():
    inv = (1.0 / np.float32(ROPE_BASE) ** (np.arange(0, HD, 2, dtype=np.float32) / np.float32(HD))).astype(np.float32)
    f = np.arange(TOKENS, dtype=np.float32)[:, None] * inv[None, :]
    c, s = np.cos(f).astype(np.float32), np.sin(f).astype(np.float32)
    t = np.concatenate([np.repeat(c, 2, axis=1), -s, s], axis=1).reshape(TILES, P, 2 * HD).transpose(1, 0, 2)
    return np.ascontiguousarray(np.concatenate([t, t], axis=1).reshape(P, -1))


def kernel(L0_attn_x, L0_attn_qkv_w, L0_attn_qkv_b, L0_attn_proj_w, L0_attn_proj_b, L0_ffn_w1_w, L0_ffn_w1_s,
           L0_ffn_w2_w, L0_ffn_w2_s, L0_ffn_h1_w, L0_ffn_h1_s, L0_ffn_h2_w, L0_ffn_h2_s, L0_ffn_w3_w, L0_ffn_w3_s):
    import concourse.bacc as bacc
    from concourse.bass_utils import run_bass_kernel_spmd

    def k_major(w):
        t = np.asarray(w).T
        return t.reshape(t.shape[0] // P, P, t.shape[1]).transpose(1, 0, 2).reshape(P, -1)

    def rows(v):
        return np.broadcast_to(np.asarray(v)[None, :], (P, np.asarray(v).shape[0]))

    def columns(v):
        return np.asarray(v).reshape(-1, P).T

    arrays = {
        "x": L0_attn_x,
        "qkv_w": k_major(L0_attn_qkv_w),
        "proj_w": k_major(L0_attn_proj_w),
        "qkv_b": rows(L0_attn_qkv_b),
        "proj_b": rows(L0_attn_proj_b),
        "ffn_w": np.concatenate([k_major(w) for w in (L0_ffn_w1_w, L0_ffn_w2_w, L0_ffn_h1_w, L0_ffn_h2_w,
                                                      L0_ffn_w3_w)], axis=1),
        "hid_s": np.concatenate([columns(s) for s in (L0_ffn_w1_s, L0_ffn_w2_s, L0_ffn_h1_s, L0_ffn_h2_s)], axis=1),
        "out_s": rows(L0_ffn_w3_s),
        "rope": rope_table(),
    }
    arrays = {n: np.ascontiguousarray(a) for n, a in arrays.items()}
    nc = bacc.Bacc("TRN2", target_bir_lowering=False, num_devices=1)
    args = [nc.dram_tensor(n, a.shape, mybir.dt.from_np(a.dtype), kind="ExternalInput").ap()
            for n, a in arrays.items()]
    out = nc.dram_tensor("out", (BATCHES, TOKENS, D), F32, kind="ExternalOutput").ap()
    build(nc, *args, out)
    r = run_bass_kernel_spmd(nc, [arrays], core_ids=[0])
    return r.results[0]["out"]
```

```python
from contextlib import ExitStack

import numpy as np

import concourse.bass as bass
from concourse import mybir

F32 = mybir.dt.float32
F32R = mybir.dt.float32r
ALU = mybir.AluOpType
ACT = mybir.ActivationFunctionType
AX_X = mybir.AxisListType.X

P = 128
BATCHES, TOKENS, D = 16, 512, 128
HEADS, HD = 16, 8
HIDDEN = 512
TILES = TOKENS // P
GROUPS, PER = 4, 4
ROWS = 32
SPLIT_ROWS = 3 * HD
SCORE_ROWS = SPLIT_ROWS + 2
KT = HIDDEN // P
EPS = 1e-5
SCALE = float(HD) ** -0.5
MASKED = -3.0e38
SLOTS = 3
UNITS = GROUPS * TILES
LAG = 2
Q_DMAS = 16 * PER
W_PIECES = 4
W_UNITS = (4, 7, 10, 13)
PRING = 4
ERING, SRING, FRING = 2, 3, 2
STEPS = UNITS * PER
ROPE_BASE = 10000.0

W_COLS = {"w1": HIDDEN, "w2": HIDDEN, "h1": KT * HIDDEN, "h2": KT * HIDDEN, "w3": KT * D}
W_AT = {}
_at = 0
for _name, _n in W_COLS.items():
    W_AT[_name] = _at
    _at += _n
W_ALL = _at

F_ORDER = [("m1", 0), ("q1", 1), ("xn", 2), ("on", -1), ("v0", 2), ("m2", 0), ("v1", 2), ("q2", 1),
           ("v2", 2), ("v3", 2), ("proj", -1), ("m3", 0), ("q3", 1), ("k0", 2), ("k1", 2), ("q0", 2),
           ("k2", 2), ("m0", 1), ("k3", 2)]
FIRST_TURN, LAST_TURN = -2, BATCHES
LOOP_FROM, LOOPS = 2, 4


def in_range(n):
    return 0 <= n < BATCHES


def f_bank(name):
    return [x for x, _ in F_ORDER].index(name) % FRING


F_USES = [sum(f_bank(x) == b for x, _ in F_ORDER) for b in range(FRING)]


def fills_before(k, bank):
    return sum(in_range(t + d) for t in range(FIRST_TURN, k) for x, d in F_ORDER if f_bank(x) == bank)


def positive(value):
    return max(value, 0) if isinstance(value, int) else value


class Turn:

    def __init__(self, j, c, looped, later=0):
        self.j, self.c, self.looped, self.later = j, c, looped, later

    def __add__(self, d):
        return Turn(self.j, self.c + d, self.looped, self.later + d)

    def exists(self):
        return self.looped or in_range(self.c)

    @property
    def n(self):
        return self.j * SLOTS + self.c if self.looped else self.c

    @property
    def slot(self):
        return self.c % SLOTS

    def count(self, per, more):
        if not self.looped:
            return positive(self.c * per + more)
        if self.later == 0:
            return self.n * per + more
        return self.j * (SLOTS * per) + (self.c * per + more)

    def filled(self, name, more=1):
        bank = f_bank(name)
        n = fills_before(self.c, bank)
        for x, d in F_ORDER:
            if x == name:
                break
            n += f_bank(x) == bank and (self.looped or in_range(self.c + d))
        n += more
        return self.j * (SLOTS * F_USES[bank]) + n if self.looped else n


def turns(eng, body):
    for c in range(FIRST_TURN, LOOP_FROM):
        body(Turn(0, c, False))
    with eng.Fori(0, LOOPS) as j:
        for c in range(SLOTS):
            body(Turn(j, LOOP_FROM + c, True))
    for c in range(LOOP_FROM + SLOTS * LOOPS, LAST_TURN + 1):
        body(Turn(0, c, False))


def build(nc, x_in, qkv_w, proj_w, qkv_b, proj_b, ffn_w, hid_s, out_s, rope, out):
    x_tiles = x_in.rearrange("b (t p) d -> b p t d", p=P)
    out_tiles = out.rearrange("b (t p) d -> b p t d", p=P)
    scratch = nc.dram_tensor("x1_scratch", (BATCHES, P, TOKENS), F32, kind="Internal").ap()

    ctx = ExitStack()
    with ctx:
        def sb(name, shape, dt=F32):
            return ctx.enter_context(nc.sbuf_tensor(name, shape, dt))

        def psum(name, shape):
            return ctx.enter_context(nc.psum_tensor(name, shape, F32))

        def sem(name):
            return ctx.enter_context(nc.semaphore(name))

        banks = psum("banks", [P, 8, 512])
        bankE = banks[:, 0:ERING]
        bankS = banks[:, ERING:ERING + SRING]
        bankF = banks[:, ERING + SRING:ERING + SRING + FRING]
        bankB = banks[:, 7]

        wqkv = sb("wqkv", [P, 3 * D])
        wproj = sb("wproj", [P, D])
        qkvb = sb("qkvb", [P, 3 * D])
        projb = sb("projb", [P, D])
        ropes = sb("ropes", [P, 2 * TILES, 2 * HD])
        ident = sb("ident", [P, P])
        ident_r = sb("ident_r", [P, P], F32R)
        later = sb("later", [P, TOKENS])
        neg_half = sb("neg_half", [P, TILES])
        hids = sb("hids", [P, 4 * KT])
        half12 = sb("half12", [P, 2 * KT])
        outs_ = sb("outs_", [P, D])

        k_cols, one_cols = SLOTS * GROUPS * TOKENS, 2 * PER * TOKENS
        arena = sb("arena", [P, k_cols + 2 * one_cols], F32R)
        kT = arena[:, 0:SLOTS * GROUPS * TOKENS].rearrange("p (s g n) -> p s g n", s=SLOTS, g=GROUPS)
        q_max = arena[:, k_cols:k_cols + one_cols].rearrange("p (r j n) -> p r j n", r=2, j=PER)
        q_exp = arena[:, k_cols + one_cols:].rearrange("p (r j n) -> p r j n", r=2, j=PER)
        flat_max = sb("flat_max", [P, TOKENS], F32R)
        flat_exp = sb("flat_exp", [P, TOKENS], F32R)
        q_cols = TILES * HEADS * ROWS
        H_COLS = KT * TOKENS
        rows = sb("rows", [P, q_cols + W_ALL + 2 * H_COLS + 2 * TOKENS], F32R)
        qrows = rows[:, 0:SLOTS * q_cols].rearrange("p (s t h r) -> p s t h r", s=SLOTS, t=TILES, h=HEADS)
        krows = rows[:, SLOTS * q_cols:(SLOTS + 1) * q_cols].rearrange("p (t h r) -> p t h r", t=TILES, h=HEADS)
        qrows_c = rows[:, 0:SLOTS * q_cols].rearrange("p (s t c) -> p s t c", s=SLOTS, t=TILES)
        krows_c = rows[:, SLOTS * q_cols:(SLOTS + 1) * q_cols].rearrange("p (t c) -> p t c", t=TILES)

        one_batch = GROUPS * TOKENS
        w_lo = arena[:, one_batch:one_batch + W_ALL]
        w_hi = rows[:, q_cols:q_cols + W_ALL]
        def hidden(buf, at):
            return buf[:, at:at + H_COLS].rearrange("p (k n) -> p k n", k=KT)

        free_a, free_r = one_batch + W_ALL, q_cols + W_ALL
        h0_hi, h0_lo, h1_hi = (hidden(arena, free_a + n * H_COLS) for n in range(3))
        h1_lo = hidden(arena, 0)
        h2_hi, h2_lo = (hidden(rows, free_r + n * H_COLS) for n in range(2))
        xt_hi = rows[:, free_r + 2 * H_COLS:free_r + 2 * H_COLS + TOKENS]
        xt_lo = rows[:, free_r + 2 * H_COLS + TOKENS:free_r + 2 * H_COLS + 2 * TOKENS]
        W_CUT = W_ALL // W_PIECES
        marks = rows[:, free_r:free_r + W_CUT]
        all_ones = rows[:, free_r + W_CUT:free_r + W_CUT + P].bitcast(F32)
        any_lo = sb("any_lo", [P, W_PIECES])
        flag_f = sb("flag_f", [1, 1])
        flag = sb("flag", [1, 1], mybir.dt.int32)

        x_ln = sb("x_ln", [P, TILES, D])
        x_res = sb("x_res", [P, TILES, D])
        v_sb = sb("v_sb", [P, SLOTS, TILES, HEADS, ROWS])
        v_flat = v_sb[:].rearrange("p s t h r -> p (s t h r)")
        stage = [v_flat[:, q_cols + n * W_CUT:q_cols + (n + 1) * W_CUT] for n in range(2)]
        probs = sb("probs", [P, PRING, PER, TOKENS])
        stats = sb("stats", [P, TILES, 6])
        meanvar = sb("meanvar", [P, TILES, 2])
        veps = sb("veps", [P, TILES])
        rstd = sb("rstd", [P, TILES])
        xn = sb("xn", [P, TILES, D])
        xnT = sb("xnT", [P, TOKENS])
        qk = sb("qk", [P, 2, TILES, D])
        rot = sb("rot", [P, 2, TILES, D])
        turned = sb("turned", [P, 2, D])
        y = sb("y", [P, TILES, D])
        rowmax = sb("rowmax", [P, TILES, HEADS])
        oT_rows = sb("oT_rows", [P, TOKENS])
        rden = sb("rden", [P, TILES, PER])
        o_tok = sb("o_tok", [P, TILES, D])
        oT = sb("oT", [P, TOKENS])
        stats_y = sb("stats_y", [P, TILES, 6])
        meanvar_y = sb("meanvar_y", [P, TILES, 2])
        veps_y = sb("veps_y", [P, TILES])
        rstd_y = sb("rstd_y", [P, TILES])
        x1 = sb("x1", [P, TILES, D])

        consts_in = sem("consts_in")
        ffn_in = sem("ffn_in")
        mask_step = sem("mask_step")
        pool_held = sem("pool_held")
        sp_held = sem("sp_held")
        dve_held = sem("dve_held")
        consts_made = sem("consts_made")
        x_in = sem("x_in")
        x_res_in = sem("x_res_in")
        ln_step = sem("ln_step")
        var_ready = sem("var_ready")
        rstd_ready = sem("rstd_ready")
        xn_ready = sem("xn_ready")
        f_full = [sem(f"f_full{r}") for r in range(FRING)]
        f_empty = [sem(f"f_empty{r}") for r in range(FRING)]
        rope_step = sem("rope_step")
        hi_ready = sem("hi_ready")
        lo_ready = sem("lo_ready")
        s_full = sem("s_full")
        s_reduced = sem("s_reduced")
        max_split = sem("max_split")
        e_full = sem("e_full")
        exp_done = sem("exp_done")
        causal_done = sem("causal_done")
        pv_done = sem("pv_done")
        oT_rows_ready = sem("oT_rows_ready")
        o_turned = sem("o_turned")
        o_normed = sem("o_normed")
        y_step = sem("y_step")
        y_var = sem("y_var")
        y_rstd = sem("y_rstd")
        x1_ready = sem("x1_ready")
        x1_stored = sem("x1_stored")
        w_in = [sem(f"w_in{n}") for n in range(W_PIECES)]
        w_hi_ready = sem("w_hi_ready")
        w_lo_ready = sem("w_lo_ready")
        marks_made = sem("marks_made")
        marked = sem("marked")
        flag_full = sem("flag_full")
        flag_ready = sem("flag_ready")
        q_max_in = [sem(f"q_max_in{r}") for r in range(2)]
        q_exp_in = [sem(f"q_exp_in{r}") for r in range(2)]

        phase_a = ExitStack()
        block = phase_a.enter_context(nc.Block())

        @block.sync
        def _(sp):
            for dst, src in ((wqkv, qkv_w), (qkvb, qkv_b), (wproj, proj_w), (projb, proj_b)):
                sp.dma_start(dst[:], src).then_inc(consts_in, 16)
            sp.dma_start(ropes[:].rearrange("p t c -> p (t c)"), rope).then_inc(consts_in, 16)

            def load_weights(k, n):
                if k.c == LAST_TURN - 1:
                    if n == 0:
                        sp.wait_ge(s_full, BATCHES * STEPS)
                        sp.wait_ge(e_full, (BATCHES - 1) * STEPS)
                        sp.wait_ge(pv_done, (BATCHES - 2) * UNITS)
                    if n == 1:
                        sp.wait_ge(pv_done, (BATCHES - 1) * UNITS)
                    if n >= 2:
                        sp.wait_ge(w_lo_ready, n - 1)
                    sp.dma_start(stage[n % 2], ffn_w[:, n * W_CUT:(n + 1) * W_CUT]).then_inc(w_in[n], 16)

            def to_exp(k, b, g):
                if b.exists():
                    sp.wait_ge(f_empty[f_bank(f"m{g}")], k.filled(f"m{g}"))
                    sp.sem_inc(sp_held, 1)
                    sp.wait_ge(e_full, b.count(STEPS, TILES * PER * (g - 1)))
                    for j in range(PER):
                        r = slice(ROWS * j, ROWS * (j + 1))
                        sp.dma_start(q_exp[r, g % 2, j, :].bitcast(F32), flat_exp[r, :].bitcast(F32)).then_inc(q_exp_in[g % 2], 16)

            def to_max(k, b, g):
                if b.exists():
                    sp.wait_ge(f_empty[f_bank(f"q{g}")], k.filled(f"q{g}"))
                    sp.sem_inc(sp_held, 1)
                    sp.wait_ge(s_full, b.count(STEPS, TILES * PER * (g - 1)))
                    for j in range(PER):
                        r = slice(ROWS * j, ROWS * (j + 1))
                        sp.dma_start(q_max[r, g % 2, j, :].bitcast(F32), flat_max[r, :].bitcast(F32)).then_inc(q_max_in[g % 2], 16)

            def turn(k):
                pre, mx, att, fin = k + 2, k + 1, k, k + -1
                load_weights(k, 0)
                if pre.exists():
                    sp.wait_ge(xn_ready, pre.count(1, 0))
                    sp.sem_inc(sp_held, 1)
                    sp.dma_start(x_ln[:], x_tiles[pre.n]).then_inc(x_in, 16)
                if fin.exists():
                    sp.wait_ge(x1_ready, fin.count(1, 0))
                    sp.sem_inc(sp_held, 1)
                    sp.dma_start(x_res[:], x_tiles[fin.n]).then_inc(x_res_in, 16)
                to_exp(k, att, 1)
                to_max(k, mx, 1)
                load_weights(k, 1)
                to_exp(k, att, 2)
                to_max(k, mx, 2)
                load_weights(k, 2)
                to_exp(k, att, 3)
                to_max(k, mx, 3)
                load_weights(k, 3)
                if k.c == FIRST_TURN:
                    sp.wait_ge(ln_step, 1)
                to_max(k, pre, 0)
                if fin.exists():
                    sp.wait_ge(x1_ready, fin.count(1, 1))
                    sp.sem_inc(sp_held, 1)
                    sp.dma_start(scratch[fin.n], x1[:].rearrange("p t d -> p (t d)")).then_inc(x1_stored, 16)
                to_exp(k, mx, 0)

            sp.dma_start(hids[:], hid_s).then_inc(ffn_in, 16)
            sp.dma_start(outs_[:], out_s).then_inc(ffn_in, 16)
            turns(sp, turn)
            sp.wait_ge(x1_stored, 16 * BATCHES)

        @block.gpsimd
        def _(pool):
            nc.gpsimd.memset(ident[:], 0.0)
            nc.gpsimd.memset(ident_r[:].bitcast(F32), 0.0)
            nc.gpsimd.memset(later[:], 0.0)
            nc.gpsimd.memset(neg_half[:], -0.5).then_inc(mask_step, 1)
            pool.wait_ge(mask_step, 1)
            for t in (ident[:], ident_r[:]):
                nc.gpsimd.affine_select(out=t, in_=t.bitcast(F32), compare_op=ALU.not_equal, fill=1.0, base=0,
                                        pattern=[[-1, P]], channel_multiplier=1)
            nc.gpsimd.affine_select(out=later[:, TOKENS - P:], in_=later[:, TOKENS - P:], compare_op=ALU.is_ge,
                                    fill=MASKED, base=0, pattern=[[-1, P]],
                                    channel_multiplier=1).then_inc(consts_made, 1)
            pool.wait_ge(consts_in, 16 * 5)
            pool.wait_ge(consts_made, 1)
            tables = ropes[:].rearrange("p (a t) c -> p a t c", a=2)

            def heads(rows_of_tile):
                return rows_of_tile.rearrange("p a (h d) -> p a h d", h=HEADS)

            def table(t, start, n):
                return tables[:, :, t, start:start + n].unsqueeze(2).to_broadcast([P, 2, HEADS, n])

            def rope_tile(k, pre, t):
                pool.wait_ge(f_empty[f_bank(f"v{t}")], k.filled(f"v{t}"))
                pool.sem_inc(pool_held, 1)
                pool.wait_ge(rope_step, pre.count(4 * TILES, 4 * t))
                source, dst, part = heads(qk[:, :, t, :]), heads(rot[:, :, t, :]), heads(turned[:])
                nc.gpsimd.tensor_tensor(part[:, :, :, 0:HD:2], source[:, :, :, 1:HD:2], table(t, HD, HD // 2),
                                        ALU.mult).then_inc(rope_step, 1)
                nc.gpsimd.tensor_tensor(part[:, :, :, 1:HD:2], source[:, :, :, 0:HD:2],
                                        table(t, HD + HD // 2, HD // 2), ALU.mult).then_inc(rope_step, 1)
                nc.gpsimd.tensor_tensor(dst, source, table(t, 0, HD), ALU.mult).then_inc(rope_step, 1)
                pool.wait_ge(rope_step, pre.count(4 * TILES, 4 * t + 3))
                nc.gpsimd.tensor_tensor(rot[:, :, t, :], rot[:, :, t, :], turned[:], ALU.add).then_inc(rope_step, 1)

            def turn(k):
                pre, att, fin = k + 2, k, k + -1
                for u in range(UNITS):
                    if u == 1 and pre.exists():
                        pool.wait_ge(var_ready, pre.count(1, 1))
                        nc.gpsimd.tensor_tensor(rstd[:], veps[:], neg_half[:], ALU.pow).then_inc(rstd_ready, 1)
                    if u == 10 and fin.exists():
                        pool.wait_ge(y_var, fin.count(1, 1))
                        nc.gpsimd.tensor_tensor(rstd_y[:], veps_y[:], neg_half[:], ALU.pow).then_inc(y_rstd, 1)
                    if att.exists():
                        pool.wait_ge(exp_done, att.count(STEPS, PER * (u + 1)))
                        pool.sem_inc(pool_held, 1)
                        diag = probs[:, (UNITS * att.c + u) % PRING, :, 0:P]
                        nc.gpsimd.affine_select(out=diag, in_=diag, compare_op=ALU.is_ge, fill=0.0, base=0,
                                                pattern=[[0, PER], [1, P]],
                                                channel_multiplier=-1).then_inc(causal_done, 1)
                    if 4 <= u < 8 and pre.exists():
                        rope_tile(k, pre, u - 4)

            turns(pool, turn)

        @block.tensor
        def _(pe):
            pe.wait_ge(consts_in, 16 * 5)
            pe.wait_ge(consts_made, 1)

            def f_free(k, name):
                pe.wait_ge(f_empty[f_bank(name)], k.filled(name, 0))

            def transposes(k, name, source):
                f_free(k, name)
                for t in range(TILES):
                    rows_in, dst = source(t), bankF[:, f_bank(name), t * P:(t + 1) * P]
                    if rows_in.dtype == F32R:
                        last = nc.tensor.transpose(dst.bitcast(F32R), rows_in, ident_r[:])
                    else:
                        last = nc.tensor.transpose(dst, rows_in, ident[:])
                last.then_inc(f_full[f_bank(name)], 1)

            def turn(k):
                pre, mx, att, fin = k + 2, k + 1, k, k + -1

                def head_rows(b, kind, g):
                    if not b.exists():
                        return
                    if kind == "m":
                        pe.wait_ge(max_split, b.count(2 * GROUPS, 2 * g + 2))
                    else:
                        pe.wait_ge(hi_ready, b.count(2, 2))
                        pe.wait_ge(lo_ready, b.count(3, 3))
                    source = krows_c if kind == "k" else qrows_c[:, b.slot]
                    transposes(k, f"{kind}{g}", lambda t: source[:, t, g * P:(g + 1) * P])

                def exp_scores(u, j):
                    if not att.exists():
                        return
                    g, kt = u // TILES, u % TILES
                    step = PER * u + j
                    if kt == 0 and j == 0:
                        pe.wait_ge(q_exp_in[g % 2], att.count(2 * Q_DMAS, Q_DMAS * (g // 2 + 1)))
                    pe.wait_ge(exp_done, att.count(STEPS, step - ERING + 1))
                    nc.tensor.matmul(bankE[:, (STEPS * att.c + step) % ERING, 0:TOKENS - kt * P],
                                     kT[:, att.slot, g, kt * P:(kt + 1) * P],
                                     q_exp[:, g % 2, j, kt * P:TOKENS], start=True, stop=True).then_inc(e_full, 1)

                def max_scores(u, j):
                    if not mx.exists():
                        return
                    g, qt = u // TILES, TILES - 1 - u % TILES
                    step = PER * u + j
                    if u % TILES == 0 and j == 0:
                        pe.wait_ge(q_max_in[g % 2], mx.count(2 * Q_DMAS, Q_DMAS * (g // 2 + 1)))
                        if g == 0:
                            pe.wait_ge(f_empty[f_bank("k3")], k.filled("m1", 0))
                    pe.wait_ge(s_reduced, mx.count(STEPS, step - SRING + 1))
                    nk = (qt + 1) * P
                    nc.tensor.matmul(bankS[:, (STEPS * mx.c + step) % SRING, 0:nk],
                                     q_max[:, g % 2, j, qt * P:nk], kT[:, mx.slot, g, 0:nk],
                                     start=True, stop=True).then_inc(s_full, 1)

                def p_v(u, j):
                    b, u = (att if u >= LAG else fin), (u - LAG) % UNITS
                    if not b.exists():
                        return
                    g, kt = u // TILES, u % TILES
                    if j == 0:
                        pe.wait_ge(causal_done, b.count(UNITS, u + 1))
                        if kt == 0:
                            pe.wait_ge(o_normed, b.count(2 * GROUPS, 2 * g))
                    last = nc.tensor.matmul(bankB[ROWS * j:ROWS * (j + 1), kt * P:TOKENS],
                                            v_sb[:, b.slot, kt, g * PER + j, :],
                                            probs[:, (UNITS * b.c + u) % PRING, j, 0:TOKENS - kt * P],
                                            start=(kt == 0), stop=(kt == TILES - 1))
                    if j == PER - 1:
                        last.then_inc(pv_done, 1)

                def turn_o(b, g):
                    if b.exists():
                        pe.wait_ge(oT_rows_ready, b.count(GROUPS, g + 1))
                        for t in range(TILES):
                            last = nc.tensor.transpose(bankB[:, t * P:(t + 1) * P],
                                                       oT_rows[:, t * P:(t + 1) * P], ident[:])
                        last.then_inc(o_turned, 1)

                def use_f(u, j):
                    if (u, j) == (0, 2):
                        head_rows(att, "m", 1)
                    if (u, j) == (1, 0):
                        head_rows(mx, "q", 1)
                    if (u, j) == (3, 0) and pre.exists():
                        pe.wait_ge(xn_ready, pre.count(1, 1))
                        transposes(k, "xn", lambda t: xn[:, t, :])
                    if (u, j) == (3, 2) and fin.exists():
                        pe.wait_ge(o_normed, fin.count(2 * GROUPS, 2 * GROUPS))
                        transposes(k, "on", lambda t: o_tok[:, t, :])
                    if (u, j) == (4, 1):
                        head_rows(att, "m", 2)
                    if (u, j) == (5, 1):
                        head_rows(mx, "q", 2)
                    if 3 <= u < 7 and j == 3 and pre.exists():
                        t = u - 3
                        if t == 0:
                            pe.wait_ge(f_empty[f_bank("xn")], k.filled("xn"))
                        f_free(k, f"v{t}")
                        b = f_bank(f"v{t}")
                        nc.tensor.matmul(bankF[:, b, 0:3 * D], xnT[:, t * P:(t + 1) * P], wqkv[:],
                                         start=True, stop=True).then_inc(f_full[b], 1)
                    if (u, j) == (7, 1) and fin.exists():
                        pe.wait_ge(f_empty[f_bank("on")], k.filled("on"))
                        f_free(k, "proj")
                        b = f_bank("proj")
                        for t in range(TILES):
                            last = nc.tensor.matmul(bankF[:, b, t * P:(t + 1) * P], oT[:, t * P:(t + 1) * P],
                                                    wproj[:], start=True, stop=True)
                        last.then_inc(f_full[b], 1)
                    if (u, j) == (8, 1):
                        head_rows(att, "m", 3)
                    if (u, j) == (9, 1):
                        head_rows(mx, "q", 3)
                    if (u, j) == (11, 1):
                        head_rows(pre, "k", 0)
                    if (u, j) == (11, 3):
                        head_rows(pre, "k", 1)
                    if (u, j) == (12, 1):
                        head_rows(pre, "q", 0)
                    if (u, j) == (12, 3):
                        head_rows(pre, "k", 2)
                    if (u, j) == (13, 1):
                        head_rows(mx, "m", 0)
                    if (u, j) == (13, 3):
                        head_rows(pre, "k", 3)

                for u in range(UNITS):
                    for j in range(PER):
                        max_scores(u, j)
                        exp_scores(u, j)
                        use_f(u, j)
                        if u % TILES == 2:
                            if j == 1:
                                turn_o(fin if u == 2 else att, (u - 6) // TILES % GROUPS)
                        elif u % TILES == 3:
                            for n in (2 * j, 2 * j + 1):
                                p_v(u - 1 + n // PER, n % PER)
                        else:
                            p_v(u, j)
                    if k.c == LAST_TURN and u == 4:
                        pe.wait_ge(marked, W_PIECES + 1)
                        nc.tensor.matmul(banks[:, 0, 0:W_PIECES], all_ones, any_lo[:], start=True,
                                         stop=True).then_inc(flag_full, 1)

            turns(pe, turn)

        @block.scalar
        def _(act):
            def leave_f(k, name, dst):
                b = f_bank(name)
                act.wait_ge(f_full[b], k.filled(name))
                nc.scalar.activation(dst, bankF[:, b], ACT.Copy).then_inc(f_empty[b], 1)

            def turn(k):
                pre, mx, att, fin = k + 2, k + 1, k, k + -1

                def exp_step(u, j):
                    if not att.exists():
                        return
                    nq, step = TOKENS - u % TILES * P, PER * u + j
                    act.wait_ge(e_full, att.count(STEPS, step + 1))
                    if j == 0:
                        act.wait_ge(pv_done, att.count(UNITS, u - PRING + 1))
                    nc.scalar.activation(probs[:, (UNITS * att.c + u) % PRING, j, 0:nq],
                                         bankE[:, (STEPS * att.c + step) % ERING, 0:nq], ACT.Exp,
                                         scale=SCALE).then_inc(exp_done, 1)

                def leave_m(b, g):
                    if b.exists():
                        act.wait_ge(q_exp_in[(g - 1) % 2],
                                    b.count(2 * Q_DMAS, Q_DMAS * ((g - 1) // 2 + 1)))
                        leave_f(k, f"m{g}", flat_exp[:])

                def leave_q(b, g):
                    if b.exists():
                        act.wait_ge(q_max_in[(g - 1) % 2],
                                    b.count(2 * Q_DMAS, Q_DMAS * ((g - 1) // 2 + 1)))
                        leave_f(k, f"q{g}", flat_max[:])

                def empty_f(u, j):
                    if (u, j) == (0, 3):
                        leave_m(att, 1)
                    if (u, j) == (1, 1):
                        leave_q(mx, 1)
                    if (u, j) == (3, 1) and pre.exists():
                        leave_f(k, "xn", xnT[:])
                    if (u, j) == (3, 3) and fin.exists():
                        leave_f(k, "on", oT[:])
                    if (u, j) == (4, 2):
                        leave_m(att, 2)
                    if (u, j) == (5, 2):
                        leave_q(mx, 2)
                    if (u, j) == (8, 2):
                        leave_m(att, 3)
                    if (u, j) == (9, 2):
                        leave_q(mx, 3)
                    if (u, j) == (11, 2) and pre.exists():
                        leave_f(k, "k0", kT[:, pre.slot, 0, :])
                    if (u, j) == (12, 0) and pre.exists():
                        leave_f(k, "k1", kT[:, pre.slot, 1, :])
                    if (u, j) == (12, 2):
                        leave_q(pre, 0)
                    if (u, j) == (13, 0) and pre.exists():
                        leave_f(k, "k2", kT[:, pre.slot, 2, :])
                    if (u, j) == (13, 2):
                        leave_m(mx, 0)
                    if (u, j) == (14, 0) and pre.exists():
                        leave_f(k, "k3", kT[:, pre.slot, 3, :])

                def high_parts(u, j):
                    if not pre.exists():
                        return
                    q_src, k_src = (rot[:, i].rearrange("p t (h d) -> p (t h) d", h=HEADS).unsqueeze(2)
                                    .to_broadcast([P, TILES * HEADS, 2, HD]) for i in range(2))
                    if (u, j) == (8, 3):
                        act.wait_ge(rope_step, pre.count(4 * TILES, 4 * TILES))
                        q_dst = qrows[:, pre.slot, :, :, 0:2 * HD].rearrange("p t h (a d) -> p (t h) a d", a=2)
                        nc.scalar.activation(q_dst, q_src, ACT.Copy).then_inc(hi_ready, 1)
                    if (u, j) == (9, 1):
                        k_dst = krows[:, :, :, 0:4 * HD].rearrange("p t h (a d) -> p (t h) a d", a=4)[:, :, 0:3:2, :]
                        nc.scalar.activation(k_dst, k_src, ACT.Copy).then_inc(hi_ready, 1)

                for u in range(UNITS):
                    done = fin if u == 2 else att
                    if u % TILES == 2 and done.exists():
                        g = (u - 6) // TILES % GROUPS
                        act.wait_ge(pv_done, done.count(UNITS, TILES * g + TILES))
                        nc.scalar.activation(oT_rows[:], bankB[:], ACT.Copy).then_inc(oT_rows_ready, 1)
                    for j in range(PER):
                        exp_step(u, j)
                        empty_f(u, j)
                        high_parts(u, j)

            act.wait_ge(ln_step, 1)
            turns(act, turn)

        @block.vector
        def _(dve):
            nc.vector.memset(rows[:, 0:(SLOTS + 1) * q_cols].bitcast(F32), 0.0)
            nc.vector.memset(arena[:, k_cols:].bitcast(F32), 0.0)
            nc.vector.memset(v_sb[:], 0.0).then_inc(consts_made, 1)
            dve.wait_ge(consts_made, 2)
            nc.vector.memset(v_sb[:].rearrange("p s t h r -> p (s t h) r")[:, :, HD:HD + 1], 1.0)
            nc.vector.memset(krows[:].rearrange("p t h r -> p (t h) r")[:, :, SPLIT_ROWS:SCORE_ROWS].bitcast(F32),
                             1.0).then_inc(ln_step, 1)
            dve.wait_ge(ln_step, 1)
            dve.wait_ge(consts_in, 16 * 5)

            def split_weights(n):
                piece = slice(n * W_CUT, (n + 1) * W_CUT)
                dve.wait_ge(w_in[n], 16)
                nc.vector.tensor_copy(w_hi[:, piece], stage[n % 2]).then_inc(w_hi_ready, 1)
                dve.wait_ge(w_hi_ready, n + 1)
                nc.vector.tensor_tensor(w_lo[:, piece], stage[n % 2], w_hi[:, piece].bitcast(F32),
                                        ALU.subtract).then_inc(w_lo_ready, 1)
                dve.wait_ge(w_lo_ready, n + 1)
                if n >= 1:
                    dve.wait_ge(marked, n + 1)
                nc.vector.tensor_scalar(marks, w_lo[:, piece].bitcast(F32), 0.0, None,
                                        ALU.not_equal).then_inc(marks_made, 1)
                dve.wait_ge(marks_made, n + 1)
                nc.vector.tensor_reduce(any_lo[:, n:n + 1], marks.bitcast(F32), AX_X, ALU.max).then_inc(marked, 1)
                if n == 0:
                    nc.vector.memset(all_ones, 1.0).then_inc(marked, 1)

            def turn(k):
                pre, mx, att, fin = k + 2, k + 1, k, k + -1

                def split_max(b, g):
                    if not b.exists():
                        return
                    src = rowmax[:, :, PER * g:PER * (g + 1)]
                    at = qrows[:, b.slot, :, PER * g:PER * (g + 1), :]
                    dve.wait_ge(s_reduced, b.count(STEPS, TILES * PER * (g + 1)))
                    nc.vector.tensor_scalar(at[:, :, :, SPLIT_ROWS], src, -1.0, None, ALU.mult).then_inc(max_split, 1)
                    dve.wait_ge(max_split, b.count(2 * GROUPS, 2 * g + 1))
                    nc.vector.scalar_tensor_tensor(out=at[:, :, :, SPLIT_ROWS + 1], in0=src, scalar=-1.0,
                                                   in1=at[:, :, :, SPLIT_ROWS].bitcast(F32), op0=ALU.mult,
                                                   op1=ALU.subtract).then_inc(max_split, 1)

                def norm_o(b, g):
                    if not b.exists():
                        return
                    dve.wait_ge(o_turned, b.count(GROUPS, g + 1))
                    turned_o = bankB[:].rearrange("p (t j r) -> p t j r", t=TILES, j=PER)
                    nc.vector.reciprocal(rden[:], turned_o[:, :, :, HD]).then_inc(o_normed, 1)
                    dve.wait_ge(o_normed, b.count(2 * GROUPS, 2 * g + 1))
                    nc.vector.tensor_tensor(
                        o_tok[:, :, g * PER * HD:(g + 1) * PER * HD].rearrange("p t (j d) -> p t j d", j=PER),
                        turned_o[:, :, :, 0:HD],
                        rden[:].unsqueeze(3).to_broadcast([P, TILES, PER, HD]), ALU.mult).then_inc(o_normed, 1)

                def prepare_tokens(u, j):
                    if u == 0:
                        if j == 0:
                            dve.wait_ge(x_in, pre.count(16, 16))
                        last = nc.vector.bn_stats(stats[:, j, :], x_ln[:, j, :])
                        if j == TILES - 1:
                            last.then_inc(ln_step, 1)
                    if (u, j) == (1, 0):
                        dve.wait_ge(ln_step, pre.count(2, 2))
                        dve.sem_inc(dve_held, 1)
                        for t in range(TILES):
                            last = nc.vector.bn_aggr(meanvar[:, t, :], stats[:, t, :])
                        last.then_inc(ln_step, 1)
                        dve.wait_ge(ln_step, pre.count(2, 3))
                        nc.vector.tensor_scalar(veps[:], meanvar[:, :, 1], EPS, None, ALU.add).then_inc(var_ready, 1)
                    if u == 2:
                        if j == 0:
                            dve.wait_ge(rstd_ready, pre.count(1, 1))
                        last = nc.vector.tensor_scalar(xn[:, j, :], x_ln[:, j, :], meanvar[:, j, 0:1],
                                                       rstd[:, j:j + 1], ALU.subtract, ALU.mult)
                        if j == TILES - 1:
                            last.then_inc(xn_ready, 1)
                    if 4 <= u < 8 and j == 0:
                        t = u - 4
                        b = f_bank(f"v{t}")
                        dve.wait_ge(f_full[b], k.filled(f"v{t}"))
                        nc.vector.tensor_tensor(qk[:, :, t, :], bankF[:, b, 0:2 * D].rearrange("p (a d) -> p a d", a=2),
                                                qkvb[:, 0:2 * D].rearrange("p (a d) -> p a d", a=2), ALU.add)
                        nc.vector.tensor_tensor(v_sb[:, pre.slot, t, :, 0:HD],
                                                bankF[:, b, 2 * D:3 * D].rearrange("p (h d) -> p h d", h=HEADS),
                                                qkvb[:, 2 * D:3 * D].rearrange("p (h d) -> p h d", h=HEADS),
                                                ALU.add).then_inc(f_empty[b], 1)
                    q_src, k_src = (rot[:, i].rearrange("p t (h d) -> p (t h) d", h=HEADS) for i in range(2))
                    q_at = qrows[:, pre.slot].rearrange("p t h r -> p (t h) r")
                    k_at = krows[:].rearrange("p t h r -> p (t h) r")
                    if (u, j) == (10, 0):
                        dve.wait_ge(hi_ready, pre.count(2, 2))
                        nc.vector.tensor_tensor(q_at[:, :, 2 * HD:3 * HD], q_src, q_at[:, :, 0:HD].bitcast(F32),
                                                ALU.subtract).then_inc(lo_ready, 1)
                    if (u, j) == (10, 2):
                        nc.vector.memset(q_at[:, :, SPLIT_ROWS:SCORE_ROWS].bitcast(F32), 0.0).then_inc(lo_ready, 1)
                    if (u, j) == (11, 0):
                        nc.vector.tensor_tensor(k_at[:, :, HD:2 * HD], k_src, k_at[:, :, 0:HD].bitcast(F32),
                                                ALU.subtract).then_inc(lo_ready, 1)

                def finish_tokens(u, j):
                    if (u, j) == (7, 3):
                        b = f_bank("proj")
                        dve.wait_ge(f_full[b], k.filled("proj"))
                        nc.vector.tensor_tensor(y[:], bankF[:, b].rearrange("p (t d) -> p t d", t=TILES),
                                                projb[:].unsqueeze(1).to_broadcast([P, TILES, D]),
                                                ALU.add).then_inc(f_empty[b], 1)
                    if u == 9:
                        if j == 0:
                            dve.wait_ge(f_empty[f_bank("proj")], k.filled("proj"))
                        last = nc.vector.bn_stats(stats_y[:, j, :], y[:, j, :])
                        if j == TILES - 1:
                            last.then_inc(y_step, 1)
                    if (u, j) == (10, 1):
                        dve.wait_ge(y_step, fin.count(3, 1))
                        dve.sem_inc(dve_held, 1)
                        for t in range(TILES):
                            last = nc.vector.bn_aggr(meanvar_y[:, t, :], stats_y[:, t, :])
                        last.then_inc(y_step, 1)
                        dve.wait_ge(y_step, fin.count(3, 2))
                        nc.vector.tensor_scalar(veps_y[:], meanvar_y[:, :, 1], EPS, None, ALU.add).then_inc(y_var, 1)
                    if u == 12:
                        if j == 0:
                            dve.wait_ge(y_rstd, fin.count(1, 1))
                        last = nc.vector.tensor_scalar(y[:, j, :], y[:, j, :], meanvar_y[:, j, 0:1],
                                                       rstd_y[:, j:j + 1], ALU.subtract, ALU.mult)
                        if j == TILES - 1:
                            last.then_inc(y_step, 1)
                    if (u, j) == (13, 1):
                        dve.wait_ge(y_step, fin.count(3, 3))
                        dve.wait_ge(x1_stored, fin.count(16, 0))
                        dve.wait_ge(x_res_in, fin.count(16, 16))
                        nc.vector.tensor_tensor(x1[:], y[:], x_res[:], ALU.add).then_inc(x1_ready, 1)

                for u in range(UNITS):
                    if u % TILES == 0:
                        split_max(att if u == 0 else mx, (u // TILES - 1) % GROUPS)
                    for j in range(PER):
                        if mx.exists():
                            g, qt, step = u // TILES, TILES - 1 - u % TILES, PER * u + j
                            dve.wait_ge(s_full, mx.count(STEPS, step + 1))
                            dve.sem_inc(dve_held, 1)
                            score = bankS[:, (STEPS * mx.c + step) % SRING, 0:(qt + 1) * P]
                            nc.vector.tensor_tensor_reduce(score, score, later[:, (TILES - 1 - qt) * P:], 1.0, MASKED,
                                                           ALU.add, ALU.max,
                                                           rowmax[:, qt, PER * g + j:PER * g + j + 1]
                                                           ).then_inc(s_reduced, 1)
                        if pre.exists():
                            prepare_tokens(u, j)
                        if fin.exists():
                            finish_tokens(u, j)
                        if u % TILES == 2 and j == 1:
                            norm_o(fin if u == 2 else att, (u - 6) // TILES % GROUPS)
                    if k.c == LAST_TURN - 1 and u in W_UNITS:
                        split_weights(W_UNITS.index(u))
                    if k.c == LAST_TURN and u == 5:
                        dve.wait_ge(flag_full, 1)
                        nc.vector.tensor_reduce(flag_f[:], banks[0:1, 0, 0:W_PIECES], AX_X,
                                                ALU.max).then_inc(flag_ready, 1)
                        dve.wait_ge(flag_ready, 1)
                        nc.vector.tensor_copy(flag[:], flag_f[:]).then_inc(flag_ready, 1)

            turns(dve, turn)

        phase_a.close()
        x1_in = sem("x1_in")
        res_in = sem("res_in")
        b_step = sem("b_step")
        b_var = sem("b_var")
        b_rstd = sem("b_rstd")
        b_xn = sem("b_xn")
        xt_full = sem("xt_full")
        xt_hi_ready = sem("xt_hi_ready")
        xt_lo_ready = sem("xt_lo_ready")
        au_full = sem("au_full")
        tanh_done = sem("tanh_done")
        gate_done = sem("gate_done")
        h0_done = sem("h0_done")
        h0_hi_ready = sem("h0_hi_ready")
        h0_lo_ready = sem("h0_lo_ready")
        layer_full = [sem("h1_full"), sem("h2_full")]
        gelu_done = [sem("h1_gelu"), sem("h2_gelu")]
        layer_lo = [sem("h1_lo_ready"), sem("h2_lo_ready")]
        w3_full = sem("w3_full")
        w3_empty = sem("w3_empty")
        c_step = sem("c_step")
        c_var = sem("c_var")
        c_rstd = sem("c_rstd")
        out_ready = sem("out_ready")
        out_stored = sem("out_stored")

        ffn_x = qk[:, 0]
        ffn_res = qk[:, 1]
        th = probs[:, 2, 0:2]
        gate = probs[:, 2, 2:4]
        h0_f = probs[:, 0]
        act_f = probs[:, 1]
        out_sb = x1
        gates = banks[:, 0:4]
        hiddens = banks[:, 4:6]
        bank_xt = banks[:, 6]

        def chunks(eng, body):
            for i in range(-2, 2):
                body(i, False)
            with eng.Fori(2, BATCHES - 3) as i:
                body(i, True)
            for i in range(BATCHES - 3, BATCHES + 1):
                body(i, False)

        def live(c, looped):
            return looped or in_range(c)

        def passes(bank, w0, k_hi, k_lo, first, last, low):
            nc.tensor.matmul(bank, w_hi[:, w0], k_hi, start=first, stop=False)
            product = nc.tensor.matmul(bank, w_hi[:, w0], k_lo, start=False, stop=last and not low)
            if low:
                product = nc.tensor.matmul(bank, w_lo[:, w0], k_hi, start=False, stop=last)
            return product

        block_b = ctx.enter_context(nc.Block())

        @block_b.sync
        def _(sp):
            def turn(i, looped):
                if live(i + 3, looped):
                    sp.wait_ge(b_xn, i + 3)
                    sp.dma_start(ffn_x.rearrange("p t d -> p (t d)"), scratch[i + 3]).then_inc(x1_in, 16)
                if live(i, looped):
                    sp.wait_ge(out_ready, i)
                    sp.dma_start(ffn_res.rearrange("p t d -> p (t d)"), scratch[i]).then_inc(res_in, 16)
                if live(i - 1, looped):
                    sp.wait_ge(out_ready, i)
                    sp.dma_start(out_tiles[i - 1], out_sb[:]).then_inc(out_stored, 16)

            sp.dma_start(ffn_x.rearrange("p t d -> p (t d)"), scratch[0]).then_inc(x1_in, 16)
            chunks(sp, turn)
            sp.wait_ge(out_stored, 16 * BATCHES)

        @block_b.gpsimd
        def _(pool):
            def turn(i, looped):
                if live(i + 2, looped):
                    pool.wait_ge(b_var, i + 3)
                    nc.gpsimd.tensor_tensor(rstd[:], veps[:], neg_half[:], ALU.pow).then_inc(b_rstd, 1)
                if live(i - 1, looped):
                    pool.wait_ge(c_var, i)
                    nc.gpsimd.tensor_tensor(rstd_y[:], veps_y[:], neg_half[:], ALU.pow).then_inc(c_rstd, 1)

            chunks(pool, turn)

        @block_b.tensor
        def _(pe):
            pe.wait_ge(w_lo_ready, W_PIECES)
            pe.wait_ge(flag_ready, 2)
            has_low = pe.value_load(flag[0:1, 0:1], min_val=0, max_val=P)

            def layer(i, number, name, src_hi, src_lo, ready, low):
                for o in range(KT):
                    if o < 2:
                        pe.wait_ge(gelu_done[1 - number], positive((i - 1 + number) * KT + o + 3))
                    else:
                        pe.wait_ge(gelu_done[number], i * KT + o - 1)
                    for k in range(KT):
                        if o == 0:
                            pe.wait_ge(ready, i * KT + (k + 1))
                        at = W_AT[name] + k * HIDDEN + o * P
                        last = passes(hiddens[:, o % 2, :], slice(at, at + P), src_hi[:, k, :], src_lo[:, k, :],
                                      k == 0, k == KT - 1, low)
                    last.then_inc(layer_full[number], 1)

            def turn(i, looped, low):
                nxt, cur, prv = live(i + 1, looped), live(i, looped), live(i - 1, looped)
                if nxt:
                    pe.wait_ge(b_xn, i + 2)
                    for t in range(TILES):
                        last = nc.tensor.transpose(bank_xt[:, t * P:(t + 1) * P], xn[:, t, :], ident[:])
                    last.then_inc(xt_full, 1)
                if cur:
                    layer(i, 0, "h1", h0_hi, h0_lo, h0_lo_ready, low)
                if prv:
                    pe.wait_ge(w3_empty, i - 1)
                    pe.wait_ge(layer_lo[1], i * KT)
                    for t in range(TILES):
                        for k in range(KT):
                            at = W_AT["w3"] + k * D
                            h_at = slice(t * P, (t + 1) * P)
                            parts = [(h2_hi, w_hi), (h2_lo, w_hi)] + [(h2_hi, w_lo)] * low
                            for n, (h, w) in enumerate(parts):
                                last = nc.tensor.matmul(bankB[:, h_at], h[:, k, h_at], w[:, at:at + D],
                                                        start=(k == 0 and n == 0),
                                                        stop=(k == KT - 1 and n == len(parts) - 1))
                    last.then_inc(w3_full, 1)
                if nxt:
                    pe.wait_ge(xt_hi_ready, i + 2)
                    pe.wait_ge(xt_lo_ready, i + 2)
                    for o in range(KT):
                        pe.wait_ge(h0_done, positive((i + 1) * KT + o - 1))
                        for half, name in ((0, "w1"), (2, "w2")):
                            at = W_AT[name] + o * P
                            last = passes(gates[:, half + o % 2, :], slice(at, at + P), xt_hi, xt_lo, True, True, low)
                        last.then_inc(au_full, 1)
                if cur:
                    layer(i, 1, "h2", h1_hi, h1_lo, layer_lo[0], low)

            with pe.If(has_low != 0):
                chunks(pe, lambda i, looped: turn(i, looped, True))
            with pe.Else():
                chunks(pe, lambda i, looped: turn(i, looped, False))

        @block_b.scalar
        def _(act):
            act.wait_ge(b_step, 2)

            def layer(i, number, hi, read_by, times):
                for o in range(KT):
                    act.wait_ge(layer_full[number], i * KT + (o + 1))
                    if o == 0:
                        act.wait_ge(read_by, times)
                    scale = hids[:, (2 + number) * KT + o:(2 + number) * KT + o + 1]
                    nc.scalar.activation(hi[:, o, :], hiddens[:, o % 2, :], ACT.Gelu, scale=scale)
                    if o < 2:
                        act.wait_ge(layer_lo[1 - number], positive((i - 1 + number) * KT + o + 3))
                    else:
                        act.wait_ge(layer_lo[number], i * KT + o - 1)
                    nc.scalar.activation(act_f[:, o % 2, :], hiddens[:, o % 2, :], ACT.Gelu,
                                         scale=scale).then_inc(gelu_done[number], 1)

            def turn(i, looped):
                nxt, cur, prv = live(i + 1, looped), live(i, looped), live(i - 1, looped)
                if nxt:
                    act.wait_ge(xt_full, i + 2)
                    nc.scalar.activation(xt_hi, bank_xt[:], ACT.Copy).then_inc(xt_hi_ready, 1)
                if cur:
                    layer(i, 0, h1_hi, layer_full[1], i * KT)
                if nxt:
                    def h0_high(o):
                        act.wait_ge(h0_done, (i + 1) * KT + (o + 1))
                        nc.scalar.activation(h0_hi[:, o, :], h0_f[:, o, :], ACT.Copy).then_inc(h0_hi_ready, 1)

                    for o in range(KT):
                        act.wait_ge(au_full, (i + 1) * KT + (o + 1))
                        act.wait_ge(gate_done, positive((i + 1) * KT + o - 1))
                        nc.scalar.activation(th[:, o % 2, :], gates[:, o % 2, :], ACT.Tanh,
                                             scale=half12[:, o:o + 1]).then_inc(tanh_done, 1)
                        if o == 0 and cur:
                            act.wait_ge(layer_full[0], (i + 1) * KT)
                        if o >= 1:
                            h0_high(o - 1)
                    h0_high(KT - 1)
                if cur:
                    layer(i, 1, h2_hi, w3_full, i)

            chunks(act, turn)

        @block_b.vector
        def _(dve):
            dve.wait_ge(ffn_in, 16 * 2)
            nc.vector.tensor_scalar(half12[:, 0:KT], hids[:, 0:KT], 0.5, None, ALU.mult).then_inc(b_step, 1)
            dve.wait_ge(b_step, 1)
            nc.vector.tensor_tensor(half12[:, KT:2 * KT], half12[:, 0:KT], hids[:, KT:2 * KT],
                                    ALU.mult).then_inc(b_step, 1)
            def layer_low(i, number, hi, lo):
                for o in range(KT):
                    dve.wait_ge(gelu_done[number], i * KT + (o + 1))
                    nc.vector.tensor_tensor(lo[:, o, :], act_f[:, o % 2, :], hi[:, o, :].bitcast(F32),
                                            ALU.subtract).then_inc(layer_lo[number], 1)

            def turn(i, looped):
                aft, nxt, cur, prv = (live(i + d, looped) for d in (2, 1, 0, -1))
                if nxt:
                    dve.wait_ge(xt_hi_ready, i + 2)
                    nc.vector.tensor_tensor(xt_lo, bank_xt[:], xt_hi.bitcast(F32), ALU.subtract).then_inc(xt_lo_ready, 1)
                if aft:
                    dve.wait_ge(x1_in, (i + 3) * 16)
                    for t in range(TILES):
                        last = nc.vector.bn_stats(stats[:, t, :], ffn_x[:, t, :])
                    last.then_inc(b_step, 1)
                    dve.wait_ge(b_step, (i + 2) * 2 + 3)
                    dve.sem_inc(dve_held, 1)
                    for t in range(TILES):
                        last = nc.vector.bn_aggr(meanvar[:, t, :], stats[:, t, :])
                    last.then_inc(b_step, 1)
                    dve.wait_ge(b_step, (i + 2) * 2 + 4)
                    nc.vector.tensor_scalar(veps[:], meanvar[:, :, 1], EPS, None, ALU.add).then_inc(b_var, 1)
                if cur:
                    layer_low(i, 0, h1_hi, h1_lo)
                if aft:
                    dve.wait_ge(b_rstd, i + 3)
                    for t in range(TILES):
                        last = nc.vector.tensor_scalar(xn[:, t, :], ffn_x[:, t, :], meanvar[:, t, 0:1],
                                                       rstd[:, t:t + 1], ALU.subtract, ALU.mult)
                    last.then_inc(b_xn, 1)
                if nxt:
                    for o in range(KT):
                        dve.wait_ge(tanh_done, (i + 1) * KT + (o + 1))
                        nc.vector.scalar_tensor_tensor(out=gate[:, o % 2, :], in0=th[:, o % 2, :], scalar=1.0,
                                                       in1=gates[:, o % 2, :], op0=ALU.add,
                                                       op1=ALU.mult).then_inc(gate_done, 1)
                        dve.wait_ge(gate_done, (i + 1) * KT + (o + 1))
                        nc.vector.scalar_tensor_tensor(out=h0_f[:, o, :], in0=gates[:, 2 + o % 2, :],
                                                       scalar=half12[:, KT + o:KT + o + 1],
                                                       in1=gate[:, o % 2, :], op0=ALU.mult,
                                                       op1=ALU.mult).then_inc(h0_done, 1)
                    for o in range(KT):
                        dve.wait_ge(h0_hi_ready, (i + 1) * KT + (o + 1))
                        nc.vector.tensor_tensor(h0_lo[:, o, :], h0_f[:, o, :], h0_hi[:, o, :].bitcast(F32),
                                                ALU.subtract).then_inc(h0_lo_ready, 1)
                if prv:
                    dve.wait_ge(out_ready, i - 1)
                    dve.wait_ge(w3_full, i)
                    nc.vector.tensor_tensor(y[:], bankB[:].rearrange("p (t d) -> p t d", t=TILES),
                                            outs_[:].unsqueeze(1).to_broadcast([P, TILES, D]),
                                            ALU.mult).then_inc(w3_empty, 1)
                    dve.wait_ge(w3_empty, i)
                    for t in range(TILES):
                        last = nc.vector.bn_stats(stats_y[:, t, :], y[:, t, :])
                    last.then_inc(c_step, 1)
                    dve.wait_ge(c_step, (i - 1) * 3 + 1)
                    dve.sem_inc(dve_held, 1)
                    for t in range(TILES):
                        last = nc.vector.bn_aggr(meanvar_y[:, t, :], stats_y[:, t, :])
                    last.then_inc(c_step, 1)
                    dve.wait_ge(c_step, (i - 1) * 3 + 2)
                    nc.vector.tensor_scalar(veps_y[:], meanvar_y[:, :, 1], EPS, None, ALU.add).then_inc(c_var, 1)
                if cur:
                    layer_low(i, 1, h2_hi, h2_lo)
                if prv:
                    dve.wait_ge(c_rstd, i)
                    for t in range(TILES):
                        last = nc.vector.tensor_scalar(y[:, t, :], y[:, t, :], meanvar_y[:, t, 0:1],
                                                       rstd_y[:, t:t + 1], ALU.subtract, ALU.mult)
                    last.then_inc(c_step, 1)
                    dve.wait_ge(c_step, (i - 1) * 3 + 3)
                    dve.wait_ge(res_in, i * 16)
                    dve.wait_ge(out_stored, (i - 1) * 16)
                    nc.vector.tensor_tensor(out_sb[:], y[:], ffn_res, ALU.add).then_inc(out_ready, 1)

            chunks(dve, turn)


def rope_table():
    inv = (1.0 / np.float32(ROPE_BASE) ** (np.arange(0, HD, 2, dtype=np.float32) / np.float32(HD))).astype(np.float32)
    f = np.arange(TOKENS, dtype=np.float32)[:, None] * inv[None, :]
    c, s = np.cos(f).astype(np.float32), np.sin(f).astype(np.float32)
    t = np.concatenate([np.repeat(c, 2, axis=1), -s, s], axis=1).reshape(TILES, P, 2 * HD).transpose(1, 0, 2)
    return np.ascontiguousarray(np.concatenate([t, t], axis=1).reshape(P, -1))


def kernel(L0_attn_x, L0_attn_qkv_w, L0_attn_qkv_b, L0_attn_proj_w, L0_attn_proj_b, L0_ffn_w1_w, L0_ffn_w1_s,
           L0_ffn_w2_w, L0_ffn_w2_s, L0_ffn_h1_w, L0_ffn_h1_s, L0_ffn_h2_w, L0_ffn_h2_s, L0_ffn_w3_w, L0_ffn_w3_s):
    import concourse.bacc as bacc
    from concourse.bass_utils import run_bass_kernel_spmd

    def k_major(w):
        t = np.asarray(w).T
        return t.reshape(t.shape[0] // P, P, t.shape[1]).transpose(1, 0, 2).reshape(P, -1)

    def rows(v):
        return np.broadcast_to(np.asarray(v)[None, :], (P, np.asarray(v).shape[0]))

    def columns(v):
        return np.asarray(v).reshape(-1, P).T

    arrays = {
        "x": L0_attn_x,
        "qkv_w": k_major(L0_attn_qkv_w),
        "proj_w": k_major(L0_attn_proj_w),
        "qkv_b": rows(L0_attn_qkv_b),
        "proj_b": rows(L0_attn_proj_b),
        "ffn_w": np.concatenate([k_major(w) for w in (L0_ffn_w1_w, L0_ffn_w2_w, L0_ffn_h1_w, L0_ffn_h2_w,
                                                      L0_ffn_w3_w)], axis=1),
        "hid_s": np.concatenate([columns(s) for s in (L0_ffn_w1_s, L0_ffn_w2_s, L0_ffn_h1_s, L0_ffn_h2_s)], axis=1),
        "out_s": rows(L0_ffn_w3_s),
        "rope": rope_table(),
    }
    arrays = {n: np.ascontiguousarray(a) for n, a in arrays.items()}
    nc = bacc.Bacc("TRN2", target_bir_lowering=False, num_devices=1)
    args = [nc.dram_tensor(n, a.shape, mybir.dt.from_np(a.dtype), kind="ExternalInput").ap()
            for n, a in arrays.items()]
    out = nc.dram_tensor("out", (BATCHES, TOKENS, D), F32, kind="ExternalOutput").ap()
    build(nc, *args, out)
    r = run_bass_kernel_spmd(nc, [arrays], core_ids=[0])
    return r.results[0]["out"]
```

```python
from contextlib import ExitStack

import numpy as np

import concourse.bass as bass
from concourse import mybir

F32 = mybir.dt.float32
F32R = mybir.dt.float32r
ALU = mybir.AluOpType
ACT = mybir.ActivationFunctionType
AX_X = mybir.AxisListType.X

P = 128
BATCHES, TOKENS, D = 16, 512, 128
HEADS, HD = 16, 8
HIDDEN = 512
TILES = TOKENS // P
GROUPS, PER = 4, 4
ROWS = 32
SPLIT_ROWS = 3 * HD
SCORE_ROWS = SPLIT_ROWS + 2
KT = HIDDEN // P
EPS = 1e-5
SCALE = float(HD) ** -0.5
MASKED = -3.0e38
SLOTS = 3
UNITS = GROUPS * TILES
LAG = 2
Q_DMAS = 16 * PER
W_PIECES = 4
P_V_LATE = (((-1, 0), (-1, 1)), ((-1, 2),), ((-1, 3),), ((0, 0),))
P_V_NEXT = (((-1, 1), (-1, 2)), ((-1, 3),), ((0, 0), (0, 1)), ((0, 2), (0, 3)))
KEY_STEPS = ((12, 2), (13, 0), (13, 3), (14, 1))
W_UNITS = (4, 7, 10, 13)
PRING = 4
ERING, SRING, FRING = 2, 3, 2
STEPS = UNITS * PER
ROPE_BASE = 10000.0

W_COLS = {"w1": HIDDEN, "w2": HIDDEN, "h1": KT * HIDDEN, "h2": KT * HIDDEN, "w3": KT * D}
W_AT = {}
_at = 0
for _name, _n in W_COLS.items():
    W_AT[_name] = _at
    _at += _n
W_ALL = _at

F_ORDER = [("m1", 0), ("q1", 1), ("on", -1), ("xn", 2), ("m2", 0), ("v0", 2), ("q2", 1), ("v1", 2),
           ("v2", 2), ("proj", -1), ("v3", 2), ("m3", 0), ("q3", 1), ("q0", 2), ("k0", 2), ("k1", 2),
           ("m0", 1), ("k2", 2), ("k3", 2)]
FIRST_TURN, LAST_TURN = -2, BATCHES
LOOP_FROM, LOOPS = 2, 4


def in_range(n):
    return 0 <= n < BATCHES


def f_bank(name):
    return [x for x, _ in F_ORDER].index(name) % FRING


F_USES = [sum(f_bank(x) == b for x, _ in F_ORDER) for b in range(FRING)]


def fills_before(k, bank):
    return sum(in_range(t + d) for t in range(FIRST_TURN, k) for x, d in F_ORDER if f_bank(x) == bank)


def positive(value):
    return max(value, 0) if isinstance(value, int) else value


class Turn:

    def __init__(self, j, c, looped, later=0):
        self.j, self.c, self.looped, self.later = j, c, looped, later

    def __add__(self, d):
        return Turn(self.j, self.c + d, self.looped, self.later + d)

    def exists(self):
        return self.looped or in_range(self.c)

    @property
    def n(self):
        return self.j * SLOTS + self.c if self.looped else self.c

    @property
    def slot(self):
        return self.c % SLOTS

    def count(self, per, more):
        if not self.looped:
            return positive(self.c * per + more)
        if self.later == 0:
            return self.n * per + more
        return self.j * (SLOTS * per) + (self.c * per + more)

    def filled(self, name, more=1):
        bank = f_bank(name)
        n = fills_before(self.c, bank)
        for x, d in F_ORDER:
            if x == name:
                break
            n += f_bank(x) == bank and (self.looped or in_range(self.c + d))
        n += more
        return self.j * (SLOTS * F_USES[bank]) + n if self.looped else n


def turns(eng, body):
    for c in range(FIRST_TURN, LOOP_FROM):
        body(Turn(0, c, False))
    with eng.Fori(0, LOOPS) as j:
        for c in range(SLOTS):
            body(Turn(j, LOOP_FROM + c, True))
    for c in range(LOOP_FROM + SLOTS * LOOPS, LAST_TURN + 1):
        body(Turn(0, c, False))


def build(nc, x_in, qkv_w, proj_w, qkv_b, proj_b, ffn_w, hid_s, out_s, rope, out):
    x_tiles = x_in.rearrange("b (t p) d -> b p t d", p=P)
    out_tiles = out.rearrange("b (t p) d -> b p t d", p=P)
    scratch = nc.dram_tensor("x1_scratch", (BATCHES, P, TOKENS), F32, kind="Internal").ap()

    ctx = ExitStack()
    with ctx:
        def sb(name, shape, dt=F32):
            return ctx.enter_context(nc.sbuf_tensor(name, shape, dt))

        def psum(name, shape):
            return ctx.enter_context(nc.psum_tensor(name, shape, F32))

        def sem(name):
            return ctx.enter_context(nc.semaphore(name))

        banks = psum("banks", [P, 8, 512])
        bankE = banks[:, 0:ERING]
        bankS = banks[:, ERING:ERING + SRING]
        bankF = banks[:, ERING + SRING:ERING + SRING + FRING]
        bankB = banks[:, 7]

        wqkv = sb("wqkv", [P, 3 * D])
        wproj = sb("wproj", [P, D])
        qkvb = sb("qkvb", [P, 3 * D])
        projb = sb("projb", [P, D])
        ropes = sb("ropes", [P, 2 * TILES, 2 * HD])
        ident = sb("ident", [P, P])
        ident_r = sb("ident_r", [P, P], F32R)
        later = sb("later", [P, TOKENS])
        neg_half = sb("neg_half", [P, TILES])
        hids = sb("hids", [P, 4 * KT])
        half12 = sb("half12", [P, 2 * KT])
        outs_ = sb("outs_", [P, D])

        k_cols, one_cols = SLOTS * GROUPS * TOKENS, 2 * PER * TOKENS
        arena = sb("arena", [P, k_cols + 2 * one_cols], F32R)
        kT = arena[:, 0:SLOTS * GROUPS * TOKENS].rearrange("p (s g n) -> p s g n", s=SLOTS, g=GROUPS)
        q_max = arena[:, k_cols:k_cols + one_cols].rearrange("p (r j n) -> p r j n", r=2, j=PER)
        q_exp = arena[:, k_cols + one_cols:].rearrange("p (r j n) -> p r j n", r=2, j=PER)
        flat_max = sb("flat_max", [P, TOKENS], F32R)
        flat_exp = sb("flat_exp", [P, TOKENS], F32R)
        q_cols = TILES * HEADS * ROWS
        H_COLS = KT * TOKENS
        rows = sb("rows", [P, q_cols + W_ALL + 2 * H_COLS + 2 * TOKENS], F32R)
        qrows = rows[:, 0:SLOTS * q_cols].rearrange("p (s t h r) -> p s t h r", s=SLOTS, t=TILES, h=HEADS)
        krows = rows[:, SLOTS * q_cols:(SLOTS + 1) * q_cols].rearrange("p (t h r) -> p t h r", t=TILES, h=HEADS)
        qrows_c = rows[:, 0:SLOTS * q_cols].rearrange("p (s t c) -> p s t c", s=SLOTS, t=TILES)
        krows_c = rows[:, SLOTS * q_cols:(SLOTS + 1) * q_cols].rearrange("p (t c) -> p t c", t=TILES)

        one_batch = GROUPS * TOKENS
        w_lo = arena[:, one_batch:one_batch + W_ALL]
        w_hi = rows[:, q_cols:q_cols + W_ALL]
        def hidden(buf, at):
            return buf[:, at:at + H_COLS].rearrange("p (k n) -> p k n", k=KT)

        free_a, free_r = one_batch + W_ALL, q_cols + W_ALL
        h0_hi, h0_lo, h1_hi = (hidden(arena, free_a + n * H_COLS) for n in range(3))
        h1_lo = hidden(arena, 0)
        h2_hi, h2_lo = (hidden(rows, free_r + n * H_COLS) for n in range(2))
        xt_hi = rows[:, free_r + 2 * H_COLS:free_r + 2 * H_COLS + TOKENS]
        xt_lo = rows[:, free_r + 2 * H_COLS + TOKENS:free_r + 2 * H_COLS + 2 * TOKENS]
        W_CUT = W_ALL // W_PIECES
        marks = rows[:, free_r:free_r + W_CUT]
        all_ones = rows[:, free_r + W_CUT:free_r + W_CUT + P].bitcast(F32)
        any_lo = sb("any_lo", [P, W_PIECES])
        flag_f = sb("flag_f", [1, 1])
        flag = sb("flag", [1, 1], mybir.dt.int32)

        x_ln = sb("x_ln", [P, TILES, D])
        x_res = sb("x_res", [P, TILES, D])
        v_sb = sb("v_sb", [P, SLOTS, TILES, HEADS, ROWS])
        v_flat = v_sb[:].rearrange("p s t h r -> p (s t h r)")
        stage = [v_flat[:, q_cols + n * W_CUT:q_cols + (n + 1) * W_CUT] for n in range(2)]
        probs = sb("probs", [P, PRING, PER, TOKENS])
        stats = sb("stats", [P, TILES, 6])
        meanvar = sb("meanvar", [P, TILES, 2])
        veps = sb("veps", [P, TILES])
        rstd = sb("rstd", [P, TILES])
        xn = sb("xn", [P, TILES, D])
        xnT = sb("xnT", [P, TOKENS])
        qk = sb("qk", [P, 2, TILES, D])
        rot = sb("rot", [P, 2, TILES, D])
        ffn_x, ffn_res = qk[:, 0], qk[:, 1]
        turned = sb("turned", [P, 2, D])
        y = sb("y", [P, TILES, D])
        rowmax = sb("rowmax", [P, TILES, HEADS])
        oT_rows = sb("oT_rows", [P, TOKENS])
        rden = sb("rden", [P, TILES, PER])
        o_tok = sb("o_tok", [P, TILES, D])
        oT = sb("oT", [P, TOKENS])
        stats_y = sb("stats_y", [P, TILES, 6])
        meanvar_y = sb("meanvar_y", [P, TILES, 2])
        veps_y = sb("veps_y", [P, TILES])
        rstd_y = sb("rstd_y", [P, TILES])
        x1 = sb("x1", [P, TILES, D])

        consts_in = sem("consts_in")
        ffn_in = sem("ffn_in")
        mask_step = sem("mask_step")
        pool_held = sem("pool_held")
        sp_held = sem("sp_held")
        dve_held = sem("dve_held")
        consts_made = sem("consts_made")
        x_in = sem("x_in")
        x_res_in = sem("x_res_in")
        ln_step = sem("ln_step")
        rings_zeroed = sem("rings_zeroed")
        var_ready = sem("var_ready")
        rstd_ready = sem("rstd_ready")
        xn_ready = sem("xn_ready")
        f_full = [sem(f"f_full{r}") for r in range(FRING)]
        f_empty = [sem(f"f_empty{r}") for r in range(FRING)]
        rope_step = sem("rope_step")
        hi_ready = sem("hi_ready")
        lo_ready = sem("lo_ready")
        s_full = sem("s_full")
        s_reduced = sem("s_reduced")
        max_split = sem("max_split")
        e_full = sem("e_full")
        exp_done = sem("exp_done")
        causal_done = sem("causal_done")
        pv_done = sem("pv_done")
        oT_rows_ready = sem("oT_rows_ready")
        o_turned = sem("o_turned")
        o_normed = sem("o_normed")
        y_step = sem("y_step")
        y_var = sem("y_var")
        y_rstd = sem("y_rstd")
        x1_ready = sem("x1_ready")
        x1_stored = sem("x1_stored")
        x1_in = sem("x1_in")
        b_step = sem("b_step")
        b_var = sem("b_var")
        b_rstd = sem("b_rstd")
        b_xn = sem("b_xn")
        w_in = [sem(f"w_in{n}") for n in range(W_PIECES)]
        w_hi_ready = sem("w_hi_ready")
        w_lo_ready = sem("w_lo_ready")
        marks_made = sem("marks_made")
        marked = sem("marked")
        flag_full = sem("flag_full")
        flag_ready = sem("flag_ready")
        q_max_in = [sem(f"q_max_in{r}") for r in range(2)]
        q_exp_in = [sem(f"q_exp_in{r}") for r in range(2)]

        phase_a = ExitStack()
        block = phase_a.enter_context(nc.Block())

        @block.sync
        def _(sp):
            for dst, src in ((wqkv, qkv_w), (qkvb, qkv_b), (wproj, proj_w), (projb, proj_b)):
                sp.dma_start(dst[:], src).then_inc(consts_in, 16)
            sp.dma_start(ropes[:].rearrange("p t c -> p (t c)"), rope).then_inc(consts_in, 16)

            def load_weights(k, n):
                if k.c == LAST_TURN - 1:
                    if n == 0:
                        sp.wait_ge(s_full, BATCHES * STEPS)
                        sp.wait_ge(e_full, (BATCHES - 1) * STEPS)
                        sp.wait_ge(pv_done, (BATCHES - 2) * UNITS)
                    if n == 1:
                        sp.wait_ge(pv_done, (BATCHES - 1) * UNITS)
                    if n >= 2:
                        sp.wait_ge(w_lo_ready, n - 1)
                    sp.dma_start(stage[n % 2], ffn_w[:, n * W_CUT:(n + 1) * W_CUT]).then_inc(w_in[n], 16)

            def to_exp(k, b, g):
                if b.exists():
                    sp.wait_ge(f_empty[f_bank(f"m{g}")], k.filled(f"m{g}"))
                    sp.sem_inc(sp_held, 1)
                    sp.wait_ge(e_full, b.count(STEPS, TILES * PER * (g - 1)))
                    for j in range(PER):
                        r = slice(ROWS * j, ROWS * (j + 1))
                        sp.dma_start(q_exp[r, g % 2, j, :].bitcast(F32), flat_exp[r, :].bitcast(F32)).then_inc(q_exp_in[g % 2], 16)

            def to_max(k, b, g):
                if b.exists():
                    sp.wait_ge(f_empty[f_bank(f"q{g}")], k.filled(f"q{g}"))
                    sp.sem_inc(sp_held, 1)
                    sp.wait_ge(s_full, b.count(STEPS, TILES * PER * (g - 1)))
                    for j in range(PER):
                        r = slice(ROWS * j, ROWS * (j + 1))
                        sp.dma_start(q_max[r, g % 2, j, :].bitcast(F32), flat_max[r, :].bitcast(F32)).then_inc(q_max_in[g % 2], 16)

            def turn(k):
                pre, mx, att, fin = k + 2, k + 1, k, k + -1
                if k.c == LAST_TURN:
                    sp.wait_ge(rope_step, BATCHES * 4 * TILES)
                    sp.wait_ge(x1_stored, 16)
                    sp.dma_start(ffn_x.rearrange("p t d -> p (t d)"), scratch[0]).then_inc(x1_in, 16)
                load_weights(k, 0)
                if pre.exists():
                    sp.wait_ge(xn_ready, pre.count(1, 0))
                    sp.sem_inc(sp_held, 1)
                    sp.dma_start(x_ln[:], x_tiles[pre.n]).then_inc(x_in, 16)
                if fin.exists():
                    sp.wait_ge(x1_ready, fin.count(1, 0))
                    sp.sem_inc(sp_held, 1)
                    sp.dma_start(x_res[:], x_tiles[fin.n]).then_inc(x_res_in, 16)
                to_exp(k, att, 1)
                to_max(k, mx, 1)
                load_weights(k, 1)
                to_exp(k, att, 2)
                to_max(k, mx, 2)
                load_weights(k, 2)
                to_exp(k, att, 3)
                to_max(k, mx, 3)
                load_weights(k, 3)
                if k.c == FIRST_TURN:
                    sp.wait_ge(rings_zeroed, 1)
                to_max(k, pre, 0)
                to_exp(k, mx, 0)
                if fin.exists():
                    sp.wait_ge(x1_ready, fin.count(1, 1))
                    sp.sem_inc(sp_held, 1)
                    sp.dma_start(scratch[fin.n], x1[:].rearrange("p t d -> p (t d)")).then_inc(x1_stored, 16)

            sp.dma_start(hids[:], hid_s).then_inc(ffn_in, 16)
            sp.dma_start(outs_[:], out_s).then_inc(ffn_in, 16)
            turns(sp, turn)

        @block.gpsimd
        def _(pool):
            nc.gpsimd.memset(ident[:], 0.0)
            nc.gpsimd.memset(ident_r[:].bitcast(F32), 0.0)
            nc.gpsimd.memset(later[:], 0.0)
            nc.gpsimd.memset(neg_half[:], -0.5).then_inc(mask_step, 1)
            pool.wait_ge(mask_step, 1)
            for t in (ident[:], ident_r[:]):
                nc.gpsimd.affine_select(out=t, in_=t.bitcast(F32), compare_op=ALU.not_equal, fill=1.0, base=0,
                                        pattern=[[-1, P]], channel_multiplier=1)
            nc.gpsimd.affine_select(out=later[:, TOKENS - P:], in_=later[:, TOKENS - P:], compare_op=ALU.is_ge,
                                    fill=MASKED, base=0, pattern=[[-1, P]],
                                    channel_multiplier=1).then_inc(consts_made, 1)
            nc.gpsimd.memset(v_sb[:], 0.0).then_inc(consts_made, 1)
            pool.wait_ge(consts_made, 2)
            nc.gpsimd.memset(v_sb[:].rearrange("p s t h r -> p (s t h) r")[:, :, HD:HD + 1], 1.0).then_inc(consts_made, 1)
            pool.wait_ge(consts_in, 16 * 5)
            tables = ropes[:].rearrange("p (a t) c -> p a t c", a=2)

            def heads(rows_of_tile):
                return rows_of_tile.rearrange("p a (h d) -> p a h d", h=HEADS)

            def table(t, start, n):
                return tables[:, :, t, start:start + n].unsqueeze(2).to_broadcast([P, 2, HEADS, n])

            def rope_tile(k, pre, t):
                pool.wait_ge(f_empty[f_bank(f"v{t}")], k.filled(f"v{t}"))
                pool.sem_inc(pool_held, 1)
                pool.wait_ge(rope_step, pre.count(4 * TILES, 4 * t))
                source, dst, part = heads(qk[:, :, t, :]), heads(rot[:, :, t, :]), heads(turned[:])
                nc.gpsimd.tensor_tensor(part[:, :, :, 0:HD:2], source[:, :, :, 1:HD:2], table(t, HD, HD // 2),
                                        ALU.mult).then_inc(rope_step, 1)
                nc.gpsimd.tensor_tensor(part[:, :, :, 1:HD:2], source[:, :, :, 0:HD:2],
                                        table(t, HD + HD // 2, HD // 2), ALU.mult).then_inc(rope_step, 1)
                nc.gpsimd.tensor_tensor(dst, source, table(t, 0, HD), ALU.mult).then_inc(rope_step, 1)
                pool.wait_ge(rope_step, pre.count(4 * TILES, 4 * t + 3))
                nc.gpsimd.tensor_tensor(rot[:, :, t, :], rot[:, :, t, :], turned[:], ALU.add).then_inc(rope_step, 1)

            def turn(k):
                pre, att, fin = k + 2, k, k + -1
                for u in range(UNITS):
                    if u == 4 and k.c == LAST_TURN:
                        pool.wait_ge(b_var, 1)
                        nc.gpsimd.tensor_tensor(rstd[:], veps[:], neg_half[:], ALU.pow).then_inc(b_rstd, 1)
                    if u == 1 and pre.exists():
                        pool.wait_ge(var_ready, pre.count(1, 1))
                        nc.gpsimd.tensor_tensor(rstd[:], veps[:], neg_half[:], ALU.pow).then_inc(rstd_ready, 1)
                    if u == 10 and fin.exists():
                        pool.wait_ge(y_var, fin.count(1, 1))
                        nc.gpsimd.tensor_tensor(rstd_y[:], veps_y[:], neg_half[:], ALU.pow).then_inc(y_rstd, 1)
                    if att.exists():
                        pool.wait_ge(exp_done, att.count(STEPS, PER * (u + 1)))
                        pool.sem_inc(pool_held, 1)
                        diag = probs[:, (UNITS * att.c + u) % PRING, :, 0:P]
                        nc.gpsimd.affine_select(out=diag, in_=diag, compare_op=ALU.is_ge, fill=0.0, base=0,
                                                pattern=[[0, PER], [1, P]],
                                                channel_multiplier=-1).then_inc(causal_done, 1)
                    if 5 <= u < 9 and pre.exists():
                        rope_tile(k, pre, u - 5)
                    if u == 13 and fin.exists():
                        pool.wait_ge(y_step, fin.count(3, 3))
                        pool.sem_inc(pool_held, 1)
                        pool.wait_ge(x1_stored, fin.count(16, 0))
                        pool.sem_inc(pool_held, 1)
                        pool.wait_ge(x_res_in, fin.count(16, 16))
                        nc.gpsimd.tensor_tensor(x1[:].rearrange("p t d -> p (t d)"), y[:].rearrange("p t d -> p (t d)"),
                                                x_res[:].rearrange("p t d -> p (t d)"), ALU.add).then_inc(x1_ready, 1)

            turns(pool, turn)

        @block.tensor
        def _(pe):
            pe.wait_ge(consts_in, 16 * 5)
            pe.wait_ge(consts_made, 1)

            def f_free(k, name):
                pe.wait_ge(f_empty[f_bank(name)], k.filled(name, 0))

            def transposes(k, name, source):
                f_free(k, name)
                for t in range(TILES):
                    rows_in, dst = source(t), bankF[:, f_bank(name), t * P:(t + 1) * P]
                    if rows_in.dtype == F32R:
                        last = nc.tensor.transpose(dst.bitcast(F32R), rows_in, ident_r[:])
                    else:
                        last = nc.tensor.transpose(dst, rows_in, ident[:])
                last.then_inc(f_full[f_bank(name)], 1)

            def turn(k):
                pre, mx, att, fin = k + 2, k + 1, k, k + -1

                def head_rows(b, kind, g):
                    if not b.exists():
                        return
                    if kind == "m":
                        pe.wait_ge(max_split, b.count(2 * GROUPS, 2 * g + 2))
                    else:
                        pe.wait_ge(hi_ready, b.count(2, 2))
                        pe.wait_ge(lo_ready, b.count(3, 3))
                    source = krows_c if kind == "k" else qrows_c[:, b.slot]
                    transposes(k, f"{kind}{g}", lambda t: source[:, t, g * P:(g + 1) * P])

                def exp_scores(u, j):
                    if not att.exists():
                        return
                    g, kt = u // TILES, u % TILES
                    step = PER * u + j
                    if kt == 0 and j == 0:
                        pe.wait_ge(q_exp_in[g % 2], att.count(2 * Q_DMAS, Q_DMAS * (g // 2 + 1)))
                    pe.wait_ge(exp_done, att.count(STEPS, step - ERING + 1))
                    nc.tensor.matmul(bankE[:, (STEPS * att.c + step) % ERING, 0:TOKENS - kt * P],
                                     kT[:, att.slot, g, kt * P:(kt + 1) * P],
                                     q_exp[:, g % 2, j, kt * P:TOKENS], start=True, stop=True).then_inc(e_full, 1)

                def max_scores(u, j):
                    if not mx.exists():
                        return
                    g, qt = u // TILES, u % TILES
                    step = PER * u + j
                    if u % TILES == 0 and j == 0:
                        pe.wait_ge(q_max_in[g % 2], mx.count(2 * Q_DMAS, Q_DMAS * (g // 2 + 1)))
                        if g == 0:
                            pe.wait_ge(f_empty[f_bank("k3")], k.filled("m1", 0))
                    pe.wait_ge(s_reduced, mx.count(STEPS, step - SRING + 1))
                    nk = (qt + 1) * P
                    nc.tensor.matmul(bankS[:, (STEPS * mx.c + step) % SRING, 0:nk],
                                     q_max[:, g % 2, j, qt * P:nk], kT[:, mx.slot, g, 0:nk],
                                     start=True, stop=True).then_inc(s_full, 1)

                def p_v(u, j):
                    b, u = (att if u >= LAG else fin), (u - LAG) % UNITS
                    if not b.exists():
                        return
                    g, kt = u // TILES, u % TILES
                    if j == 0:
                        pe.wait_ge(causal_done, b.count(UNITS, u + 1))
                        if kt == 0:
                            pe.wait_ge(o_normed, b.count(2 * GROUPS, 2 * g))
                    last = nc.tensor.matmul(bankB[ROWS * j:ROWS * (j + 1), kt * P:TOKENS],
                                            v_sb[:, b.slot, kt, g * PER + j, :],
                                            probs[:, (UNITS * b.c + u) % PRING, j, 0:TOKENS - kt * P],
                                            start=(kt == 0), stop=(kt == TILES - 1))
                    if j == PER - 1:
                        last.then_inc(pv_done, 1)

                def turn_o(b, g):
                    if b.exists():
                        pe.wait_ge(oT_rows_ready, b.count(GROUPS, g + 1))
                        for t in range(TILES):
                            last = nc.tensor.transpose(bankB[:, t * P:(t + 1) * P],
                                                       oT_rows[:, t * P:(t + 1) * P], ident[:])
                        last.then_inc(o_turned, 1)

                def use_f(u, j):
                    if (u, j) == (0, 2):
                        head_rows(att, "m", 1)
                    if (u, j) == (1, 0):
                        head_rows(mx, "q", 1)
                    if (u, j) == (3, 2) and fin.exists():
                        pe.wait_ge(o_normed, fin.count(2 * GROUPS, 2 * GROUPS))
                        transposes(k, "on", lambda t: o_tok[:, t, :])
                    if (u, j) == (4, 0) and pre.exists():
                        pe.wait_ge(xn_ready, pre.count(1, 1))
                        transposes(k, "xn", lambda t: xn[:, t, :])
                    if (u, j) == (4, 1):
                        head_rows(att, "m", 2)
                    if (u, j) == (5, 1):
                        head_rows(mx, "q", 2)
                    if (u, j) == (7, 1) and fin.exists():
                        pe.wait_ge(f_empty[f_bank("on")], k.filled("on"))
                        f_free(k, "proj")
                        b = f_bank("proj")
                        for t in range(TILES):
                            last = nc.tensor.matmul(bankF[:, b, t * P:(t + 1) * P], oT[:, t * P:(t + 1) * P],
                                                    wproj[:], start=True, stop=True)
                        last.then_inc(f_full[b], 1)
                    if 4 <= u < 8 and j == 3 and pre.exists():
                        t = u - 4
                        if t == 0:
                            pe.wait_ge(f_empty[f_bank("xn")], k.filled("xn"))
                        f_free(k, f"v{t}")
                        b = f_bank(f"v{t}")
                        nc.tensor.matmul(bankF[:, b, 0:3 * D], xnT[:, t * P:(t + 1) * P], wqkv[:],
                                         start=True, stop=True).then_inc(f_full[b], 1)
                    if (u, j) == (8, 1):
                        head_rows(att, "m", 3)
                    if (u, j) == (9, 1):
                        head_rows(mx, "q", 3)
                    if (u, j) == (12, 0):
                        head_rows(pre, "q", 0)
                    if (u, j) == (12, 2):
                        head_rows(pre, "k", 0)
                    if (u, j) == (13, 0):
                        head_rows(pre, "k", 1)
                    if (u, j) == (13, 1):
                        head_rows(mx, "m", 0)
                    if (u, j) == (13, 3):
                        head_rows(pre, "k", 2)
                    if (u, j) == (14, 1):
                        head_rows(pre, "k", 3)

                for u in range(UNITS):
                    for j in range(PER):
                        max_scores(u, j)
                        exp_scores(u, j)
                        use_f(u, j)
                        if u % TILES == 2:
                            if j == 1:
                                turn_o(fin if u == 2 else att, (u - 6) // TILES % GROUPS)
                        elif u % TILES == 3:
                            for unit, head in P_V_LATE[j]:
                                p_v(u + unit, head)
                        elif u % TILES == 0:
                            for unit, head in P_V_NEXT[j]:
                                p_v(u + unit, head)
                        else:
                            p_v(u, j)
                    if k.c == LAST_TURN and u == 4:
                        pe.wait_ge(marked, W_PIECES + 1)
                        nc.tensor.matmul(banks[:, 0, 0:W_PIECES], all_ones, any_lo[:], start=True,
                                         stop=True).then_inc(flag_full, 1)

            turns(pe, turn)

        @block.scalar
        def _(act):
            def leave_f(k, name, dst):
                b = f_bank(name)
                act.wait_ge(f_full[b], k.filled(name))
                nc.scalar.activation(dst, bankF[:, b], ACT.Copy).then_inc(f_empty[b], 1)

            def turn(k):
                pre, mx, att, fin = k + 2, k + 1, k, k + -1

                def exp_step(u, j):
                    if not att.exists():
                        return
                    nq, step = TOKENS - u % TILES * P, PER * u + j
                    act.wait_ge(e_full, att.count(STEPS, step + 1))
                    if j == 0:
                        act.wait_ge(pv_done, att.count(UNITS, u - PRING + 1))
                    nc.scalar.activation(probs[:, (UNITS * att.c + u) % PRING, j, 0:nq],
                                         bankE[:, (STEPS * att.c + step) % ERING, 0:nq], ACT.Exp,
                                         scale=SCALE).then_inc(exp_done, 1)

                def leave_m(b, g):
                    if b.exists():
                        act.wait_ge(q_exp_in[(g - 1) % 2],
                                    b.count(2 * Q_DMAS, Q_DMAS * ((g - 1) // 2 + 1)))
                        leave_f(k, f"m{g}", flat_exp[:])

                def leave_q(b, g):
                    if b.exists():
                        act.wait_ge(q_max_in[(g - 1) % 2],
                                    b.count(2 * Q_DMAS, Q_DMAS * ((g - 1) // 2 + 1)))
                        leave_f(k, f"q{g}", flat_max[:])

                def empty_f(u, j):
                    if (u, j) == (0, 3):
                        leave_m(att, 1)
                    if (u, j) == (1, 1):
                        leave_q(mx, 1)
                    if (u, j) == (3, 3) and fin.exists():
                        leave_f(k, "on", oT[:])
                    if (u, j) == (4, 1) and pre.exists():
                        leave_f(k, "xn", xnT[:])
                    if (u, j) == (4, 2):
                        leave_m(att, 2)
                    if (u, j) == (5, 2):
                        leave_q(mx, 2)
                    if (u, j) == (8, 2):
                        leave_m(att, 3)
                    if (u, j) == (9, 2):
                        leave_q(mx, 3)
                    if (u, j) == (12, 1):
                        leave_q(pre, 0)
                    if (u, j) == (13, 2):
                        leave_m(mx, 0)

                def high_parts(u, j):
                    if not pre.exists():
                        return
                    q_src, k_src = (rot[:, i].rearrange("p t (h d) -> p (t h) d", h=HEADS).unsqueeze(2)
                                    .to_broadcast([P, TILES * HEADS, 2, HD]) for i in range(2))
                    if (u, j) == (10, 0):
                        act.wait_ge(rope_step, pre.count(4 * TILES, 4 * TILES))
                        q_dst = qrows[:, pre.slot, :, :, 0:2 * HD].rearrange("p t h (a d) -> p (t h) a d", a=2)
                        nc.scalar.activation(q_dst, q_src, ACT.Copy).then_inc(hi_ready, 1)
                    if (u, j) == (10, 3):
                        k_dst = krows[:, :, :, 0:4 * HD].rearrange("p t h (a d) -> p (t h) a d", a=4)[:, :, 0:3:2, :]
                        nc.scalar.activation(k_dst, k_src, ACT.Copy).then_inc(hi_ready, 1)

                for u in range(UNITS):
                    done = fin if u == 2 else att
                    if u % TILES == 2 and done.exists():
                        g = (u - 6) // TILES % GROUPS
                        act.wait_ge(pv_done, done.count(UNITS, TILES * g + TILES))
                        nc.scalar.activation(oT_rows[:], bankB[:], ACT.Copy).then_inc(oT_rows_ready, 1)
                    for j in range(PER):
                        exp_step(u, j)
                        empty_f(u, j)
                        high_parts(u, j)

            act.wait_ge(consts_made, 1)
            for at in range(k_cols, k_cols + 2 * one_cols, 4 * TOKENS):
                last = nc.scalar.activation(arena[:, at:at + 4 * TOKENS], later[:, 0:1].to_broadcast([P, 4 * TOKENS]),
                                            ACT.Copy)
            last.then_inc(rings_zeroed, 1)
            act.wait_ge(ln_step, 1)
            turns(act, turn)

        @block.vector
        def _(dve):
            all_rows = rows[:, 0:(SLOTS + 1) * q_cols].rearrange("p (h r) -> p h r", r=ROWS)
            nc.vector.memset(all_rows[:, :, SCORE_ROWS:].bitcast(F32), 0.0)
            nc.vector.memset(krows[:].rearrange("p t h r -> p (t h) r")[:, :, SPLIT_ROWS:SCORE_ROWS].bitcast(F32),
                             1.0).then_inc(ln_step, 1)
            dve.wait_ge(ln_step, 1)
            dve.wait_ge(consts_made, 3)
            dve.wait_ge(consts_in, 16 * 5)

            def first_chunk(u):
                if u == 4:
                    dve.wait_ge(x1_in, 16)
                    for t in range(TILES):
                        last = nc.vector.bn_stats(stats[:, t, :], ffn_x[:, t, :])
                    last.then_inc(b_step, 1)
                    dve.wait_ge(b_step, 1)
                    dve.sem_inc(dve_held, 1)
                    for t in range(TILES):
                        last = nc.vector.bn_aggr(meanvar[:, t, :], stats[:, t, :])
                    last.then_inc(b_step, 1)
                    dve.wait_ge(b_step, 2)
                    nc.vector.tensor_scalar(veps[:], meanvar[:, :, 1], EPS, None, ALU.add).then_inc(b_var, 1)
                if u == 11:
                    dve.wait_ge(b_rstd, 1)
                    for t in range(TILES):
                        last = nc.vector.tensor_scalar(xn[:, t, :], ffn_x[:, t, :], meanvar[:, t, 0:1],
                                                       rstd[:, t:t + 1], ALU.subtract, ALU.mult)
                    last.then_inc(b_xn, 1)

            def split_weights(n):
                piece = slice(n * W_CUT, (n + 1) * W_CUT)
                dve.wait_ge(w_in[n], 16)
                nc.vector.tensor_copy(w_hi[:, piece], stage[n % 2]).then_inc(w_hi_ready, 1)
                dve.wait_ge(w_hi_ready, n + 1)
                nc.vector.tensor_tensor(w_lo[:, piece], stage[n % 2], w_hi[:, piece].bitcast(F32),
                                        ALU.subtract).then_inc(w_lo_ready, 1)
                dve.wait_ge(w_lo_ready, n + 1)
                if n >= 1:
                    dve.wait_ge(marked, n + 1)
                nc.vector.tensor_scalar(marks, w_lo[:, piece].bitcast(F32), 0.0, None,
                                        ALU.not_equal).then_inc(marks_made, 1)
                dve.wait_ge(marks_made, n + 1)
                nc.vector.tensor_reduce(any_lo[:, n:n + 1], marks.bitcast(F32), AX_X, ALU.max).then_inc(marked, 1)
                if n == 0:
                    nc.vector.memset(all_ones, 1.0).then_inc(marked, 1)

            def turn(k):
                pre, mx, att, fin = k + 2, k + 1, k, k + -1

                def split_max(b, g):
                    if not b.exists():
                        return
                    src = rowmax[:, :, PER * g:PER * (g + 1)]
                    at = qrows[:, b.slot, :, PER * g:PER * (g + 1), :]
                    dve.wait_ge(s_reduced, b.count(STEPS, TILES * PER * (g + 1)))
                    nc.vector.tensor_scalar(at[:, :, :, SPLIT_ROWS], src, -1.0, None, ALU.mult).then_inc(max_split, 1)
                    dve.wait_ge(max_split, b.count(2 * GROUPS, 2 * g + 1))
                    nc.vector.scalar_tensor_tensor(out=at[:, :, :, SPLIT_ROWS + 1], in0=src, scalar=-1.0,
                                                   in1=at[:, :, :, SPLIT_ROWS].bitcast(F32), op0=ALU.mult,
                                                   op1=ALU.subtract).then_inc(max_split, 1)

                def norm_o(b, g):
                    if not b.exists():
                        return
                    dve.wait_ge(o_turned, b.count(GROUPS, g + 1))
                    turned_o = bankB[:].rearrange("p (t j r) -> p t j r", t=TILES, j=PER)
                    nc.vector.reciprocal(rden[:], turned_o[:, :, :, HD]).then_inc(o_normed, 1)
                    dve.wait_ge(o_normed, b.count(2 * GROUPS, 2 * g + 1))
                    nc.vector.tensor_tensor(
                        o_tok[:, :, g * PER * HD:(g + 1) * PER * HD].rearrange("p t (j d) -> p t j d", j=PER),
                        turned_o[:, :, :, 0:HD],
                        rden[:].unsqueeze(3).to_broadcast([P, TILES, PER, HD]), ALU.mult).then_inc(o_normed, 1)

                def leave_f(name, dst):
                    b = f_bank(name)
                    dve.wait_ge(f_full[b], k.filled(name))
                    nc.vector.tensor_copy(dst, bankF[:, b]).then_inc(f_empty[b], 1)

                def prepare_tokens(u, j):
                    if u == 0:
                        if j == 0:
                            dve.wait_ge(x_in, pre.count(16, 16))
                        last = nc.vector.bn_stats(stats[:, j, :], x_ln[:, j, :])
                        if j == TILES - 1:
                            last.then_inc(ln_step, 1)
                    if (u, j) == (1, 0):
                        dve.wait_ge(ln_step, pre.count(2, 2))
                        dve.sem_inc(dve_held, 1)
                        for t in range(TILES):
                            last = nc.vector.bn_aggr(meanvar[:, t, :], stats[:, t, :])
                        last.then_inc(ln_step, 1)
                        dve.wait_ge(ln_step, pre.count(2, 3))
                        nc.vector.tensor_scalar(veps[:], meanvar[:, :, 1], EPS, None, ALU.add).then_inc(var_ready, 1)
                    if u == 2:
                        if j == 0:
                            dve.wait_ge(rstd_ready, pre.count(1, 1))
                        last = nc.vector.tensor_scalar(xn[:, j, :], x_ln[:, j, :], meanvar[:, j, 0:1],
                                                       rstd[:, j:j + 1], ALU.subtract, ALU.mult)
                        if j == TILES - 1:
                            last.then_inc(xn_ready, 1)
                    if 5 <= u < 9 and j == 0:
                        t = u - 5
                        b = f_bank(f"v{t}")
                        dve.wait_ge(f_full[b], k.filled(f"v{t}"))
                        nc.vector.tensor_tensor(qk[:, :, t, :], bankF[:, b, 0:2 * D].rearrange("p (a d) -> p a d", a=2),
                                                qkvb[:, 0:2 * D].rearrange("p (a d) -> p a d", a=2), ALU.add)
                        nc.vector.tensor_tensor(v_sb[:, pre.slot, t, :, 0:HD],
                                                bankF[:, b, 2 * D:3 * D].rearrange("p (h d) -> p h d", h=HEADS),
                                                qkvb[:, 2 * D:3 * D].rearrange("p (h d) -> p h d", h=HEADS),
                                                ALU.add).then_inc(f_empty[b], 1)
                    q_src, k_src = (rot[:, i].rearrange("p t (h d) -> p (t h) d", h=HEADS) for i in range(2))
                    q_at = qrows[:, pre.slot].rearrange("p t h r -> p (t h) r")
                    k_at = krows[:].rearrange("p t h r -> p (t h) r")
                    if (u, j) == (11, 0):
                        dve.wait_ge(hi_ready, pre.count(2, 2))
                        nc.vector.tensor_tensor(q_at[:, :, 2 * HD:3 * HD], q_src, q_at[:, :, 0:HD].bitcast(F32),
                                                ALU.subtract).then_inc(lo_ready, 1)
                    if (u, j) == (10, 2):
                        nc.vector.memset(q_at[:, :, SPLIT_ROWS:SCORE_ROWS].bitcast(F32), 0.0).then_inc(lo_ready, 1)
                    if (u, j) == (11, 1):
                        nc.vector.tensor_tensor(k_at[:, :, HD:2 * HD], k_src, k_at[:, :, 0:HD].bitcast(F32),
                                                ALU.subtract).then_inc(lo_ready, 1)

                    if (u, j) in KEY_STEPS:
                        n = KEY_STEPS.index((u, j))
                        leave_f(f"k{n}", kT[:, pre.slot, n, :])

                def finish_tokens(u, j):
                    if (u, j) == (7, 3):
                        dve.wait_ge(x1_ready, fin.count(1, 0))
                        b = f_bank("proj")
                        dve.wait_ge(f_full[b], k.filled("proj"))
                        nc.vector.tensor_tensor(y[:], bankF[:, b].rearrange("p (t d) -> p t d", t=TILES),
                                                projb[:].unsqueeze(1).to_broadcast([P, TILES, D]),
                                                ALU.add).then_inc(f_empty[b], 1)
                    if u == 9:
                        if j == 0:
                            dve.wait_ge(f_empty[f_bank("proj")], k.filled("proj"))
                        last = nc.vector.bn_stats(stats_y[:, j, :], y[:, j, :])
                        if j == TILES - 1:
                            last.then_inc(y_step, 1)
                    if (u, j) == (10, 1):
                        dve.wait_ge(y_step, fin.count(3, 1))
                        dve.sem_inc(dve_held, 1)
                        for t in range(TILES):
                            last = nc.vector.bn_aggr(meanvar_y[:, t, :], stats_y[:, t, :])
                        last.then_inc(y_step, 1)
                        dve.wait_ge(y_step, fin.count(3, 2))
                        nc.vector.tensor_scalar(veps_y[:], meanvar_y[:, :, 1], EPS, None, ALU.add).then_inc(y_var, 1)
                    if u == 12:
                        if j == 0:
                            dve.wait_ge(y_rstd, fin.count(1, 1))
                        last = nc.vector.tensor_scalar(y[:, j, :], y[:, j, :], meanvar_y[:, j, 0:1],
                                                       rstd_y[:, j:j + 1], ALU.subtract, ALU.mult)
                        if j == TILES - 1:
                            last.then_inc(y_step, 1)

                for u in range(UNITS):
                    if u % TILES == 0:
                        split_max(att if u == 0 else mx, (u // TILES - 1) % GROUPS)
                    for j in range(PER):
                        if mx.exists():
                            g, qt, step = u // TILES, u % TILES, PER * u + j
                            dve.wait_ge(s_full, mx.count(STEPS, step + 1))
                            dve.sem_inc(dve_held, 1)
                            score = bankS[:, (STEPS * mx.c + step) % SRING, 0:(qt + 1) * P]
                            nc.vector.tensor_tensor_reduce(score, score, later[:, (TILES - 1 - qt) * P:], 1.0, MASKED,
                                                           ALU.add, ALU.max,
                                                           rowmax[:, qt, PER * g + j:PER * g + j + 1]
                                                           ).then_inc(s_reduced, 1)
                        if pre.exists():
                            prepare_tokens(u, j)
                        if fin.exists():
                            finish_tokens(u, j)
                        if u % TILES == 2 and j == 1:
                            norm_o(fin if u == 2 else att, (u - 6) // TILES % GROUPS)
                    if k.c == LAST_TURN - 1 and u in W_UNITS:
                        split_weights(W_UNITS.index(u))
                    if k.c == LAST_TURN:
                        first_chunk(u)
                    if k.c == LAST_TURN and u == 5:
                        dve.wait_ge(flag_full, 1)
                        nc.vector.tensor_reduce(flag_f[:], banks[0:1, 0, 0:W_PIECES], AX_X,
                                                ALU.max).then_inc(flag_ready, 1)
                        dve.wait_ge(flag_ready, 1)
                        nc.vector.tensor_copy(flag[:], flag_f[:]).then_inc(flag_ready, 1)

            turns(dve, turn)

        phase_a.close()
        res_in = sem("res_in")
        xt_full = sem("xt_full")
        xt_hi_ready = sem("xt_hi_ready")
        xt_lo_ready = sem("xt_lo_ready")
        au_full = sem("au_full")
        tanh_done = sem("tanh_done")
        gate_done = sem("gate_done")
        h0_done = sem("h0_done")
        h0_hi_ready = sem("h0_hi_ready")
        h0_lo_ready = sem("h0_lo_ready")
        layer_full = [sem("h1_full"), sem("h2_full")]
        gelu_done = [sem("h1_gelu"), sem("h2_gelu")]
        layer_lo = [sem("h1_lo_ready"), sem("h2_lo_ready")]
        w3_full = sem("w3_full")
        w3_empty = sem("w3_empty")
        c_step = sem("c_step")
        c_var = sem("c_var")
        c_rstd = sem("c_rstd")
        out_ready = sem("out_ready")
        out_stored = sem("out_stored")

        th = probs[:, 2, 0:2]
        gate = probs[:, 2, 2:4]
        h0_f = probs[:, 0]
        act_f = probs[:, 1]
        out_sb = x1
        gates = banks[:, 0:4]
        hiddens = banks[:, 4:6]
        bank_xt = banks[:, 6]

        def chunks(eng, body):
            for i in range(-1, 2):
                body(i, False)
            with eng.Fori(2, BATCHES - 3) as i:
                body(i, True)
            for i in range(BATCHES - 3, BATCHES + 1):
                body(i, False)

        def live(c, looped):
            return looped or in_range(c)

        def passes(bank, w0, k_hi, k_lo, first, last, low):
            nc.tensor.matmul(bank, w_hi[:, w0], k_hi, start=first, stop=False)
            product = nc.tensor.matmul(bank, w_hi[:, w0], k_lo, start=False, stop=last and not low)
            if low:
                product = nc.tensor.matmul(bank, w_lo[:, w0], k_hi, start=False, stop=last)
            return product

        block_b = ctx.enter_context(nc.Block())

        @block_b.sync
        def _(sp):
            def turn(i, looped):
                if live(i + 3, looped):
                    sp.wait_ge(b_xn, i + 3)
                    sp.dma_start(ffn_x.rearrange("p t d -> p (t d)"), scratch[i + 3]).then_inc(x1_in, 16)
                if live(i, looped):
                    sp.wait_ge(out_ready, i)
                    sp.dma_start(ffn_res.rearrange("p t d -> p (t d)"), scratch[i]).then_inc(res_in, 16)
                if live(i - 1, looped):
                    sp.wait_ge(out_ready, i)
                    sp.dma_start(out_tiles[i - 1], out_sb[:]).then_inc(out_stored, 16)

            sp.wait_ge(x1_stored, 16 * BATCHES)
            sp.wait_ge(b_xn, 1)
            sp.dma_start(ffn_x.rearrange("p t d -> p (t d)"), scratch[1]).then_inc(x1_in, 16)
            chunks(sp, turn)
            sp.wait_ge(out_stored, 16 * BATCHES)

        @block_b.gpsimd
        def _(pool):
            def turn(i, looped):
                if live(i + 2, looped):
                    pool.wait_ge(b_var, i + 3)
                    nc.gpsimd.tensor_tensor(rstd[:], veps[:], neg_half[:], ALU.pow).then_inc(b_rstd, 1)
                if live(i - 1, looped):
                    pool.wait_ge(c_var, i)
                    nc.gpsimd.tensor_tensor(rstd_y[:], veps_y[:], neg_half[:], ALU.pow).then_inc(c_rstd, 1)
                if live(i - 1, looped):
                    pool.wait_ge(c_step, (i - 1) * 3 + 3)
                    pool.wait_ge(res_in, i * 16)
                    pool.wait_ge(out_stored, (i - 1) * 16)
                    nc.gpsimd.tensor_tensor(out_sb[:].rearrange("p t d -> p (t d)"),
                                            y[:].rearrange("p t d -> p (t d)"),
                                            ffn_res.rearrange("p t d -> p (t d)"), ALU.add).then_inc(out_ready, 1)
                if live(i + 1, looped):
                    for o in range(KT):
                        pool.wait_ge(h0_hi_ready, (i + 1) * KT + (o + 1))
                        nc.gpsimd.tensor_tensor(h0_lo[:, o, :], h0_f[:, o, :], h0_hi[:, o, :].bitcast(F32),
                                                ALU.subtract).then_inc(h0_lo_ready, 1)

            chunks(pool, turn)

        @block_b.tensor
        def _(pe):
            pe.wait_ge(w_lo_ready, W_PIECES)
            pe.wait_ge(flag_ready, 2)
            has_low = pe.value_load(flag[0:1, 0:1], min_val=0, max_val=P)

            def layer(i, number, name, src_hi, src_lo, ready, low, o):
                if o < 2:
                    pe.wait_ge(gelu_done[1 - number], positive((i - 1 + number) * KT + o + 3))
                else:
                    pe.wait_ge(gelu_done[number], i * KT + o - 1)
                for k in range(KT):
                    if o == 0:
                        pe.wait_ge(ready, i * KT + (k + 1))
                    at = W_AT[name] + k * HIDDEN + o * P
                    last = passes(hiddens[:, o % 2, :], slice(at, at + P), src_hi[:, k, :], src_lo[:, k, :],
                                  k == 0, k == KT - 1, low)
                last.then_inc(layer_full[number], 1)

            def turn(i, looped, low):
                nxt, cur, prv = live(i + 1, looped), live(i, looped), live(i - 1, looped)

                def h1(o):
                    if cur:
                        layer(i, 0, "h1", h0_hi, h0_lo, h0_lo_ready, low, o)

                def h2(o):
                    if cur:
                        layer(i, 1, "h2", h1_hi, h1_lo, layer_lo[0], low, o)

                def gated(o):
                    if nxt:
                        if o == 0:
                            pe.wait_ge(xt_hi_ready, i + 2)
                            pe.wait_ge(xt_lo_ready, i + 2)
                        pe.wait_ge(h0_done, positive((i + 1) * KT + o - 1))
                        for half, name in ((0, "w1"), (2, "w2")):
                            at = W_AT[name] + o * P
                            last = passes(gates[:, half + o % 2, :], slice(at, at + P), xt_hi, xt_lo, True, True, low)
                        last.then_inc(au_full, 1)

                if nxt:
                    pe.wait_ge(b_xn, i + 2)
                    for t in range(TILES):
                        last = nc.tensor.transpose(bank_xt[:, t * P:(t + 1) * P], xn[:, t, :], ident[:])
                    last.then_inc(xt_full, 1)
                h1(0)
                h1(1)
                if prv:
                    pe.wait_ge(w3_empty, i - 1)
                    pe.wait_ge(layer_lo[1], i * KT)
                    for t in range(TILES):
                        for k in range(KT):
                            at = W_AT["w3"] + k * D
                            h_at = slice(t * P, (t + 1) * P)
                            parts = [(h2_hi, w_hi), (h2_lo, w_hi)] + [(h2_hi, w_lo)] * low
                            for n, (h, w) in enumerate(parts):
                                last = nc.tensor.matmul(bankB[:, h_at], h[:, k, h_at], w[:, at:at + D],
                                                        start=(k == 0 and n == 0),
                                                        stop=(k == KT - 1 and n == len(parts) - 1))
                    last.then_inc(w3_full, 1)
                h1(2)
                h1(3)
                gated(0)
                gated(1)
                h2(0)
                gated(2)
                h2(1)
                gated(3)
                h2(2)
                h2(3)

            with pe.If(has_low != 0):
                chunks(pe, lambda i, looped: turn(i, looped, True))
            with pe.Else():
                chunks(pe, lambda i, looped: turn(i, looped, False))

        @block_b.scalar
        def _(act):
            act.wait_ge(b_step, 4)

            def layer(i, number, hi, read_by, times, o):
                act.wait_ge(layer_full[number], i * KT + (o + 1))
                if o == 0:
                    act.wait_ge(read_by, times)
                scale = hids[:, (2 + number) * KT + o:(2 + number) * KT + o + 1]
                nc.scalar.activation(hi[:, o, :], hiddens[:, o % 2, :], ACT.Gelu, scale=scale)
                if o < 2:
                    act.wait_ge(layer_lo[1 - number], positive((i - 1 + number) * KT + o + 3))
                else:
                    act.wait_ge(layer_lo[number], i * KT + o - 1)
                nc.scalar.activation(act_f[:, o % 2, :], hiddens[:, o % 2, :], ACT.Gelu,
                                     scale=scale).then_inc(gelu_done[number], 1)

            def turn(i, looped):
                nxt, cur, prv = live(i + 1, looped), live(i, looped), live(i - 1, looped)

                def h2(o):
                    if cur:
                        layer(i, 1, h2_hi, w3_full, i, o)

                def gated(o):
                    if nxt:
                        act.wait_ge(au_full, (i + 1) * KT + (o + 1))
                        act.wait_ge(gate_done, positive((i + 1) * KT + o - 1))
                        nc.scalar.activation(th[:, o % 2, :], gates[:, o % 2, :], ACT.Tanh,
                                             scale=half12[:, o:o + 1]).then_inc(tanh_done, 1)

                def h0_high(o):
                    if nxt:
                        act.wait_ge(h0_done, (i + 1) * KT + (o + 1))
                        nc.scalar.activation(h0_hi[:, o, :], h0_f[:, o, :], ACT.Copy).then_inc(h0_hi_ready, 1)

                if nxt:
                    act.wait_ge(xt_full, i + 2)
                    nc.scalar.activation(xt_hi, bank_xt[:], ACT.Copy).then_inc(xt_hi_ready, 1)
                if cur:
                    for o in range(KT):
                        layer(i, 0, h1_hi, layer_full[1], i * KT, o)
                gated(0)
                if nxt and cur:
                    act.wait_ge(layer_full[0], (i + 1) * KT)
                gated(1)
                h0_high(0)
                h2(0)
                gated(2)
                h0_high(1)
                h2(1)
                gated(3)
                h0_high(2)
                h2(2)
                h0_high(3)
                h2(3)

            chunks(act, turn)

        @block_b.vector
        def _(dve):
            dve.wait_ge(ffn_in, 16 * 2)
            nc.vector.tensor_scalar(half12[:, 0:KT], hids[:, 0:KT], 0.5, None, ALU.mult).then_inc(b_step, 1)
            dve.wait_ge(b_step, 3)
            nc.vector.tensor_tensor(half12[:, KT:2 * KT], half12[:, 0:KT], hids[:, KT:2 * KT],
                                    ALU.mult).then_inc(b_step, 1)
            def layer_low(i, number, hi, lo, o):
                dve.wait_ge(gelu_done[number], i * KT + (o + 1))
                nc.vector.tensor_tensor(lo[:, o, :], act_f[:, o % 2, :], hi[:, o, :].bitcast(F32),
                                        ALU.subtract).then_inc(layer_lo[number], 1)

            def turn(i, looped):
                aft, nxt, cur, prv = (live(i + d, looped) for d in (2, 1, 0, -1))

                def h1_low(o):
                    if cur:
                        layer_low(i, 0, h1_hi, h1_lo, o)

                def h2_low(o):
                    if cur:
                        layer_low(i, 1, h2_hi, h2_lo, o)

                def gated(o):
                    if nxt:
                        dve.wait_ge(tanh_done, (i + 1) * KT + (o + 1))
                        nc.vector.scalar_tensor_tensor(out=gate[:, o % 2, :], in0=th[:, o % 2, :], scalar=1.0,
                                                       in1=gates[:, o % 2, :], op0=ALU.add,
                                                       op1=ALU.mult).then_inc(gate_done, 1)
                        if o == 0 and cur:
                            dve.wait_ge(h0_lo_ready, (i + 1) * KT)
                        dve.wait_ge(gate_done, (i + 1) * KT + (o + 1))
                        nc.vector.scalar_tensor_tensor(out=h0_f[:, o, :], in0=gates[:, 2 + o % 2, :],
                                                       scalar=half12[:, KT + o:KT + o + 1],
                                                       in1=gate[:, o % 2, :], op0=ALU.mult,
                                                       op1=ALU.mult).then_inc(h0_done, 1)

                if nxt:
                    dve.wait_ge(xt_hi_ready, i + 2)
                    nc.vector.tensor_tensor(xt_lo, bank_xt[:], xt_hi.bitcast(F32), ALU.subtract).then_inc(xt_lo_ready, 1)
                if aft:
                    dve.wait_ge(x1_in, (i + 3) * 16)
                    for t in range(TILES):
                        last = nc.vector.bn_stats(stats[:, t, :], ffn_x[:, t, :])
                    last.then_inc(b_step, 1)
                    dve.wait_ge(b_step, (i + 2) * 2 + 3)
                    dve.sem_inc(dve_held, 1)
                    for t in range(TILES):
                        last = nc.vector.bn_aggr(meanvar[:, t, :], stats[:, t, :])
                    last.then_inc(b_step, 1)
                    dve.wait_ge(b_step, (i + 2) * 2 + 4)
                    nc.vector.tensor_scalar(veps[:], meanvar[:, :, 1], EPS, None, ALU.add).then_inc(b_var, 1)
                h1_low(0)
                h1_low(1)
                if prv:
                    dve.wait_ge(out_ready, i - 1)
                    dve.wait_ge(w3_full, i)
                    nc.vector.tensor_tensor(y[:], bankB[:].rearrange("p (t d) -> p t d", t=TILES),
                                            outs_[:].unsqueeze(1).to_broadcast([P, TILES, D]),
                                            ALU.mult).then_inc(w3_empty, 1)
                    dve.wait_ge(w3_empty, i)
                    for t in range(TILES):
                        last = nc.vector.bn_stats(stats_y[:, t, :], y[:, t, :])
                    last.then_inc(c_step, 1)
                    dve.wait_ge(c_step, (i - 1) * 3 + 1)
                    dve.sem_inc(dve_held, 1)
                    for t in range(TILES):
                        last = nc.vector.bn_aggr(meanvar_y[:, t, :], stats_y[:, t, :])
                    last.then_inc(c_step, 1)
                    dve.wait_ge(c_step, (i - 1) * 3 + 2)
                    nc.vector.tensor_scalar(veps_y[:], meanvar_y[:, :, 1], EPS, None, ALU.add).then_inc(c_var, 1)
                h1_low(2)
                if aft:
                    dve.wait_ge(b_rstd, i + 3)
                    for t in range(TILES):
                        last = nc.vector.tensor_scalar(xn[:, t, :], ffn_x[:, t, :], meanvar[:, t, 0:1],
                                                       rstd[:, t:t + 1], ALU.subtract, ALU.mult)
                    last.then_inc(b_xn, 1)
                h1_low(3)
                gated(0)
                if prv:
                    dve.wait_ge(c_rstd, i)
                    for t in range(TILES):
                        last = nc.vector.tensor_scalar(y[:, t, :], y[:, t, :], meanvar_y[:, t, 0:1],
                                                       rstd_y[:, t:t + 1], ALU.subtract, ALU.mult)
                    last.then_inc(c_step, 1)
                gated(1)
                h2_low(0)
                gated(2)
                h2_low(1)
                gated(3)
                h2_low(2)
                h2_low(3)

            chunks(dve, turn)


def rope_table():
    inv = (1.0 / np.float32(ROPE_BASE) ** (np.arange(0, HD, 2, dtype=np.float32) / np.float32(HD))).astype(np.float32)
    f = np.arange(TOKENS, dtype=np.float32)[:, None] * inv[None, :]
    c, s = np.cos(f).astype(np.float32), np.sin(f).astype(np.float32)
    t = np.concatenate([np.repeat(c, 2, axis=1), -s, s], axis=1).reshape(TILES, P, 2 * HD).transpose(1, 0, 2)
    return np.ascontiguousarray(np.concatenate([t, t], axis=1).reshape(P, -1))


def kernel(L0_attn_x, L0_attn_qkv_w, L0_attn_qkv_b, L0_attn_proj_w, L0_attn_proj_b, L0_ffn_w1_w, L0_ffn_w1_s,
           L0_ffn_w2_w, L0_ffn_w2_s, L0_ffn_h1_w, L0_ffn_h1_s, L0_ffn_h2_w, L0_ffn_h2_s, L0_ffn_w3_w, L0_ffn_w3_s):
    import concourse.bacc as bacc
    from concourse.bass_utils import run_bass_kernel_spmd

    def k_major(w):
        t = np.asarray(w).T
        return t.reshape(t.shape[0] // P, P, t.shape[1]).transpose(1, 0, 2).reshape(P, -1)

    def rows(v):
        return np.broadcast_to(np.asarray(v)[None, :], (P, np.asarray(v).shape[0]))

    def columns(v):
        return np.asarray(v).reshape(-1, P).T

    arrays = {
        "x": L0_attn_x,
        "qkv_w": k_major(L0_attn_qkv_w),
        "proj_w": k_major(L0_attn_proj_w),
        "qkv_b": rows(L0_attn_qkv_b),
        "proj_b": rows(L0_attn_proj_b),
        "ffn_w": np.concatenate([k_major(w) for w in (L0_ffn_w1_w, L0_ffn_w2_w, L0_ffn_h1_w, L0_ffn_h2_w,
                                                      L0_ffn_w3_w)], axis=1),
        "hid_s": np.concatenate([columns(s) for s in (L0_ffn_w1_s, L0_ffn_w2_s, L0_ffn_h1_s, L0_ffn_h2_s)], axis=1),
        "out_s": rows(L0_ffn_w3_s),
        "rope": rope_table(),
    }
    arrays = {n: np.ascontiguousarray(a) for n, a in arrays.items()}
    nc = bacc.Bacc("TRN2", target_bir_lowering=False, num_devices=1)
    args = [nc.dram_tensor(n, a.shape, mybir.dt.from_np(a.dtype), kind="ExternalInput").ap()
            for n, a in arrays.items()]
    out = nc.dram_tensor("out", (BATCHES, TOKENS, D), F32, kind="ExternalOutput").ap()
    build(nc, *args, out)
    r = run_bass_kernel_spmd(nc, [arrays], core_ids=[0])
    return r.results[0]["out"]
```
